# Optimizing a Trainium2 kernel written in Bass

```python
import numpy as np
import jax
import jax.numpy as jnp

def _softmax(x, axis=-1):
    return jax.nn.softmax(x, axis=axis)

def _gelu(x):
    return jax.nn.gelu(x, approximate=True)

def _silu(x):
    return jax.nn.silu(x)

def _sigmoid(x):
    return jax.nn.sigmoid(x)

def _layernorm(x, axis=-1, eps=1e-05):
    m = jnp.mean(x, axis=axis, keepdims=True)
    v = jnp.var(x, axis=axis, keepdims=True)
    return (x - m) / jnp.sqrt(v + eps)

def _scatter_add(tgt, idx, src, axis=0):
    return tgt.at[idx].add(src)

def _segment_sum(src, seg, n):
    return jax.ops.segment_sum(src, seg, n)
kernel_name = 'mk_adj_resnorm_d4_adj_r2_68ecdd'

def setup_inputs(seed: int=0):
    np.random.seed(seed)
    _w = jnp.asarray

    def _rec_inputs():
        import jax
        import jax.numpy as jnp
        _gk = jax.random.key(seed)
        x = -0.0005207 + 1.001 * jax.random.normal(jax.random.fold_in(_gk, 1), (32, 256, 128), jnp.float32)
        _w = (1.0 + jnp.arange(256, dtype=jnp.float32)) ** (-0.5)
        _w = _w / _w.mean()
        _pij = jnp.clip(0.0625 * _w[:, None] * _w[None, :], 0.0, 1.0)
        _a = jax.random.uniform(jax.random.fold_in(_gk, 2), (32, 256, 256)) < _pij
        _af = _a.astype(jnp.float32)
        adj = _af
        return (x, adj)
    x, adj = _rec_inputs()

    def _L0_gnn_setup():
        import jax, jax.numpy as jnp
        import numpy as np
        DIM = 128
        HEADS = 8
        BS = 8
        N = 512
        NEG = -1000000000.0
        key = jax.random.key(seed)
        ks = jax.random.split(key, 8)
        feats = jax.random.normal(ks[0], (BS, N, DIM), dtype=jnp.float32)
        adj_mat = (jax.random.uniform(ks[1], (BS, N, N)) < 0.1).astype(jnp.float32)
        s = 1.0 / np.sqrt(DIM)
        fc_w = jax.random.normal(ks[2], (DIM, DIM * HEADS), dtype=jnp.float32) * s
        fc_b = jnp.zeros((DIM * HEADS,), dtype=jnp.float32)
        q_w = jax.random.normal(ks[3], (DIM, 1), dtype=jnp.float32) * s
        q_b = jnp.zeros((1,), dtype=jnp.float32)
        k_w = jax.random.normal(ks[4], (DIM, 1), dtype=jnp.float32) * s
        k_b = jnp.zeros((1,), dtype=jnp.float32)
        fp_w = jax.random.normal(ks[5], (DIM * HEADS, DIM), dtype=jnp.float32) * (1.0 / np.sqrt(DIM * HEADS))
        fp_b = jnp.zeros((DIM,), dtype=jnp.float32)
        return {'feats': feats, 'adj_mat': adj_mat, 'fc_w': fc_w, 'fc_b': fc_b, 'q_w': q_w, 'q_b': q_b, 'k_w': k_w, 'k_b': k_b, 'fp_w': fp_w, 'fp_b': fp_b}
    _L0_gnn_all = _L0_gnn_setup()
    _L0_gnn_in = {k: v for k, v in _L0_gnn_all.items() if k in ('fc_w', 'fc_b', 'q_w', 'q_b', 'k_w', 'k_b', 'fp_w', 'fp_b')}
    del _L0_gnn_all

    def _L1_gnn_setup():
        import jax, jax.numpy as jnp
        import numpy as np
        D_IN = 128
        D_HID = 256
        key = jax.random.key(seed)
        k1, k2, k3, k4, k5, k6 = jax.random.split(key, 6)
        x = jax.random.normal(k1, (8, 2048, D_IN), dtype=jnp.float32)
        adj = jax.random.uniform(k2, (8, 2048, 2048), dtype=jnp.float32)
        s1 = 1.0 / np.sqrt(D_IN)
        s2 = 1.0 / np.sqrt(D_HID)
        W1 = jax.random.uniform(k3, (D_IN, D_HID), dtype=jnp.float32, minval=-s1, maxval=s1)
        b1 = jax.random.uniform(k4, (D_HID,), dtype=jnp.float32, minval=-s1, maxval=s1)
        W2 = jax.random.uniform(k5, (D_HID, D_IN), dtype=jnp.float32, minval=-s2, maxval=s2)
        b2 = jax.random.uniform(k6, (D_IN,), dtype=jnp.float32, minval=-s2, maxval=s2)
        eps = jnp.zeros((1,), dtype=jnp.float32)
        return {'x': x, 'adj': adj, 'eps': eps, 'W1': W1, 'b1': b1, 'W2': W2, 'b2': b2}
    _L1_gnn_all = _L1_gnn_setup()
    _L1_gnn_in = {k: v for k, v in _L1_gnn_all.items() if k in ('eps', 'W1', 'b1', 'W2', 'b2')}
    del _L1_gnn_all

    def _L2_gnn_setup():
        import jax, jax.numpy as jnp
        import numpy as np
        B, N, D, H = (8, 1024, 128, 512)
        RMS_EPS = 1e-06

        def _rmsnorm(h, w, eps=RMS_EPS):
            var = jnp.mean(jnp.square(h), axis=-1, keepdims=True)
            return h * jax.lax.rsqrt(var + eps) * w
        key = jax.random.key(seed)
        ks = jax.random.split(key, 5)
        x = jax.random.normal(ks[0], (B, N, D), dtype=jnp.float32)
        adjacency = jax.random.uniform(ks[1], (B, N, N), dtype=jnp.float32)
        epsilon = jnp.zeros((), dtype=jnp.float32)
        W1 = jax.random.normal(ks[2], (D, H), dtype=jnp.float32) * (1.0 / np.sqrt(D))
        b1 = jnp.zeros((H,), dtype=jnp.float32)
        rms_weight = jnp.ones((H,), dtype=jnp.float32)
        W2 = jax.random.normal(ks[3], (H, D), dtype=jnp.float32) * (1.0 / np.sqrt(H))
        b2 = jnp.zeros((D,), dtype=jnp.float32)
        return {'x': x, 'adjacency': adjacency, 'epsilon': epsilon, 'W1': W1, 'b1': b1, 'rms_weight': rms_weight, 'W2': W2, 'b2': b2}
    _L2_gnn_all = _L2_gnn_setup()
    _L2_gnn_in = {k: v for k, v in _L2_gnn_all.items() if k in ('epsilon', 'W1', 'b1', 'rms_weight', 'W2', 'b2')}
    del _L2_gnn_all

    def _L3_gnn_setup():
        import jax, jax.numpy as jnp
        import numpy as np
        B, N, IN_DIM, OUT_DIM, H = (8, 512, 128, 128, 4)
        D = OUT_DIM // H
        NEG_INF = -9000000000000000.0
        LRELU_SLOPE = 0.2
        key = jax.random.key(seed)
        k1, k2, k3, k4 = jax.random.split(key, 4)
        x = jax.random.normal(k1, (B, N, IN_DIM), dtype=jnp.float32)
        adj = jax.random.randint(k2, (B, N, N), 0, 2).astype(jnp.float32)
        W = jax.random.normal(k3, (IN_DIM, H * D), dtype=jnp.float32) * jnp.sqrt(2.0 / (IN_DIM + H * D))
        a = jax.random.normal(k4, (H, 2 * D), dtype=jnp.float32) * jnp.sqrt(2.0 / (H + 2 * D))
        return {'x': x, 'adj': adj, 'W': W, 'a': a}
    _L3_gnn_all = _L3_gnn_setup()
    _L3_gnn_in = {k: v for k, v in _L3_gnn_all.items() if k in ('W', 'a')}
    del _L3_gnn_all
    return {'x': x, 'adj': adj, 'L0_gnn_fc_w': _L0_gnn_in['fc_w'], 'L0_gnn_fc_b': _L0_gnn_in['fc_b'], 'L0_gnn_q_w': _L0_gnn_in['q_w'], 'L0_gnn_q_b': _L0_gnn_in['q_b'], 'L0_gnn_k_w': _L0_gnn_in['k_w'], 'L0_gnn_k_b': _L0_gnn_in['k_b'], 'L0_gnn_fp_w': _L0_gnn_in['fp_w'], 'L0_gnn_fp_b': _L0_gnn_in['fp_b'], 'L1_gnn_eps': _L1_gnn_in['eps'], 'L1_gnn_W1': _L1_gnn_in['W1'], 'L1_gnn_b1': _L1_gnn_in['b1'], 'L1_gnn_W2': _L1_gnn_in['W2'], 'L1_gnn_b2': _L1_gnn_in['b2'], 'L2_gnn_epsilon': _L2_gnn_in['epsilon'], 'L2_gnn_W1': _L2_gnn_in['W1'], 'L2_gnn_b1': _L2_gnn_in['b1'], 'L2_gnn_rms_weight': _L2_gnn_in['rms_weight'], 'L2_gnn_W2': _L2_gnn_in['W2'], 'L2_gnn_b2': _L2_gnn_in['b2'], 'L3_gnn_W': _L3_gnn_in['W'], 'L3_gnn_a': _L3_gnn_in['a']}

def reference(x, adj, L0_gnn_fc_w, L0_gnn_fc_b, L0_gnn_q_w, L0_gnn_q_b, L0_gnn_k_w, L0_gnn_k_b, L0_gnn_fp_w, L0_gnn_fp_b, L1_gnn_eps, L1_gnn_W1, L1_gnn_b1, L1_gnn_W2, L1_gnn_b2, L2_gnn_epsilon, L2_gnn_W1, L2_gnn_b1, L2_gnn_rms_weight, L2_gnn_W2, L2_gnn_b2, L3_gnn_W, L3_gnn_a):
    import jax
    import jax.numpy as jnp

    def _L0_gnn_ref(feats, adj_mat, fc_w, fc_b, q_w, q_b, k_w, k_b, fp_w, fp_b):
        import jax, jax.numpy as jnp
        import numpy as np
        DIM = 128
        HEADS = 8
        BS = 8
        N = 512
        NEG = -1000000000.0
        bs, n, dim = feats.shape
        feat_proj = (feats @ fc_w + fc_b).reshape(bs, n, HEADS, dim).transpose(0, 2, 1, 3)
        q = feat_proj @ q_w + q_b
        k = feat_proj @ k_w + k_b
        logits = q + jnp.swapaxes(k, -1, -2)
        masked = logits + (1.0 - adj_mat[:, None]) * NEG
        masked = jax.nn.leaky_relu(masked, negative_slope=0.01)
        attn = jax.nn.softmax(masked, axis=-1)
        out = attn @ feat_proj
        out = out.transpose(0, 2, 1, 3).reshape(bs, n, HEADS * dim)
        out = out @ fp_w + fp_b + feats
        return jax.nn.sigmoid(out)

    def _L1_gnn_ref(x, adj, eps, W1, b1, W2, b2):
        import jax, jax.numpy as jnp
        import numpy as np
        D_IN = 128
        D_HID = 256
        aggregated = jnp.einsum('bnm,bmd->bnd', adj, x)
        h = (1.0 + eps) * x + aggregated
        h = jax.nn.relu(h @ W1 + b1)
        return h @ W2 + b2

    def _L2_gnn_ref(x, adjacency, epsilon, W1, b1, rms_weight, W2, b2):
        import jax, jax.numpy as jnp
        import numpy as np
        B, N, D, H = (8, 1024, 128, 512)
        RMS_EPS = 1e-06

        def _rmsnorm(h, w, eps=RMS_EPS):
            var = jnp.mean(jnp.square(h), axis=-1, keepdims=True)
            return h * jax.lax.rsqrt(var + eps) * w
        neighbor_sum = jnp.einsum('bnm,bmd->bnd', adjacency, x)
        agg = epsilon * x + neighbor_sum
        h = jnp.einsum('bnd,dh->bnh', agg, W1) + b1
        h = jax.nn.silu(_rmsnorm(h, rms_weight))
        out = jnp.einsum('bnh,hd->bnd', h, W2) + b2
        return out

    def _L3_gnn_ref(x, adj, W, a):
        import jax, jax.numpy as jnp
        import numpy as np
        B, N, IN_DIM, OUT_DIM, H = (8, 512, 128, 128, 4)
        D = OUT_DIM // H
        NEG_INF = -9000000000000000.0
        LRELU_SLOPE = 0.2
        h = jnp.einsum('bni,io->bno', x, W).reshape(x.shape[0], x.shape[1], H, D)
        h = h.transpose(0, 2, 1, 3)
        a1, a2 = (a[:, :D], a[:, D:])
        e_i = jnp.einsum('bhnd,hd->bhn', h, a1)
        e_j = jnp.einsum('bhmd,hd->bhm', h, a2)
        e = e_i[:, :, :, None] + e_j[:, :, None, :]
        e = jnp.where(e > 0, e, LRELU_SLOPE * e)
        e = jnp.where(adj[:, None, :, :] > 0, e, NEG_INF)
        attn = jax.nn.softmax(e, axis=-1)
        out = jnp.einsum('bhnm,bhmd->bhnd', attn, h)
        out = out.transpose(0, 2, 1, 3).reshape(x.shape[0], x.shape[1], H * D)
        return out
    x = _layernorm(x + _L0_gnn_ref(x, adj, L0_gnn_fc_w, L0_gnn_fc_b, L0_gnn_q_w, L0_gnn_q_b, L0_gnn_k_w, L0_gnn_k_b, L0_gnn_fp_w, L0_gnn_fp_b), axis=-1)
    x = _layernorm(x + _L1_gnn_ref(x, adj, L1_gnn_eps, L1_gnn_W1, L1_gnn_b1, L1_gnn_W2, L1_gnn_b2), axis=-1)
    x = _layernorm(x + _L2_gnn_ref(x, adj, L2_gnn_epsilon, L2_gnn_W1, L2_gnn_b1, L2_gnn_rms_weight, L2_gnn_W2, L2_gnn_b2), axis=-1)
    x = _layernorm(x + _L3_gnn_ref(x, adj, L3_gnn_W, L3_gnn_a), axis=-1)
    return x

_drawn_inputs = setup_inputs


def setup_inputs(seed=0):
    import zlib

    import numpy as np

    out = dict(_drawn_inputs(seed))
    spreads = {'L0_gnn_fc_b': (0.0, 0.1),
     'L0_gnn_fp_b': (0.0, 0.1),
     'L2_gnn_b1': (0.0, 0.8),
     'L2_gnn_rms_weight': (1.0, 0.2),
     'L2_gnn_b2': (0.0, 0.1)}
    factors = {'L0_gnn_q_w': 4.28, 'L1_gnn_b1': 3.132}
    for name, (base, spread) in spreads.items():
        noise = np.random.default_rng([zlib.crc32(name.encode()), seed]).standard_normal(out[name].shape)
        drawn = base * np.exp(spread * noise) if base else spread * noise
        out[name] = jnp.asarray(drawn.astype(out[name].dtype))
    for name, factor in factors.items():
        out[name] = (out[name] * factor).astype(out[name].dtype)
    return out
```

```python
from contextlib import ExitStack

import concourse.bass as bass
from concourse import mybir

ALU = mybir.AluOpType
ACT = mybir.ActivationFunctionType
AX = mybir.AxisListType
F32 = mybir.dt.float32
F16 = mybir.dt.float16
BF16 = mybir.dt.bfloat16

P = 128
H0, H3 = 8, 4
A0, A3 = 0.01, 0.2
D3 = P // H3
HID1, HID2 = 256, 512
LN_EPS, RMS_EPS = 1e-5, 1e-6
CLAMP = 60.0
BIG = 2.0 ** 127
FLOOR = 2.0 ** -80
GV = P + 1
GROUPS = ((0, 3), (3, 6), (6, 8))
UNITS = [(g, nb) for g in range(3) for nb in range(2)]
NO = 3

SKEW = dict(A=0, B=1, P=2, C=3, D=4, E=5, F=6)
DEPTH = max(SKEW.values())
RING = 8

PHASES = [
    ("A_xT", "A"), ("A_adjT", "A"), ("D_agg", "D"),
    ("D_h0", "D"), ("E_xT", "E"), ("D_h1", "D"),
    ("F_V", "F"), ("A_rows", "A"), ("C_agg", "C"),
    ("E_rows", "E"), ("F_O", "F"), ("D_t0", "D"),
    ("C_h", "C"), ("A_E", "A"), ("D_t1", "D"),
    ("E_E", "E"), ("C_y", "C"), ("D_y", "D"),
]
NMID = 3
INDEX = {name: k for k, (name, _) in enumerate(PHASES)}


class Signals:

    def __init__(self, new):
        def each(name, n):
            return [new(f"{name}{k}") for k in range(n)]

        self.weights_loaded = new("weights_loaded")
        self.ident_zero, self.ident_ready = new("ident_zero"), new("ident_ready")
        self.turned, self.turned_read, self.folded = new("turned"), new("turned_read"), new("folded")
        self.ablk_zero, self.ablk_ready = new("ablk_zero"), new("ablk_ready")
        self.qk_summed, self.constants_ready = new("qk_summed"), new("constants_ready")
        self.x_loaded, self.adj_loaded = new("x_loaded"), new("adj_loaded")
        self.xT_done, self.xT_ready = new("xT_done"), new("xT_ready")
        self.adjT_done, self.adjT_ready, self.limit_ready = new("adjT_done"), new("adjT_ready"), new("limit_ready")
        self.rows_done, self.rows_read = new("rows_done"), new("rows_read")
        self.kmax_done, self.kq_done = new("kmax_done"), new("kq_done")
        self.rowR_ready, self.rowE_ready = new("rowR_ready"), new("rowE_ready")
        self.R_stored, self.R_loaded = new("R_stored"), new("R_loaded")
        self.E_done, self.E_ready = new("E_done"), new("E_ready")
        self.val_done, self.val_ready = each("val_done", 4), each("val_ready", 4)
        self.edge_done, self.weight_ready = each("edge_done", 4), each("weight_ready", 4)
        self.xbias_ready = new("xbias_ready")
        self.attn_done, self.attn_sum, self.attn_read = each("attn_done", 6), each("attn_sum", 6), each("attn_read", 6)
        self.tree1_done, self.tree2_done, self.tree3_done = new("tree1_done"), new("tree2_done"), new("tree3_done")
        self.zsum_ready, self.sg0_ready = new("zsum_ready"), new("sg0_ready")
        self.x1_hi_done, self.x1_split, self.x1b_ready = new("x1_hi_done"), new("x1_split"), new("x1b_ready")
        self.agg1_done, self.agg1_ready = new("agg1_done"), new("agg1_ready")
        self.hid1_done, self.hid1_ready, self.y1_done = new("hid1_done"), new("hid1_ready"), new("y1_done")
        self.x2_hi_done, self.x2_split, self.x2b_ready = new("x2_hi_done"), new("x2_split"), new("x2b_ready")
        self.agg2_done, self.agg2_ready = new("agg2_done"), new("agg2_ready")
        self.hid2_done, self.hid2_ready = each("hid2_done", 2), each("hid2_ready", 2)
        self.sumsq_done, self.gate_done = each("sumsq_done", 2), each("gate_done", 2)
        self.msq_done, self.rms_done, self.half_done = new("msq_done"), new("rms_done"), new("half_done")
        self.tanh_done, self.sil_done = each("tanh_done", 2), each("sil_done", 2)
        self.silT_done, self.silT_ready = each("silT_done", 2), each("silT_ready", 2)
        self.y2_done = new("y2_done")
        self.x3T_done, self.x3T_ready = new("x3T_done"), new("x3T_ready")
        self.rows3_done, self.kmax3_done, self.rows3_read = new("rows3_done"), new("kmax3_done"), new("rows3_read")
        self.rowR3_ready, self.rowE3_ready = new("rowR3_ready"), new("rowE3_ready")
        self.R3_stored, self.R3_loaded = new("R3_stored"), new("R3_loaded")
        self.E3_done, self.E3_ready = new("E3_done"), new("E3_ready")
        self.V3_done, self.V3_ready = new("V3_done"), new("V3_ready")
        self.edge3_done, self.weight3_ready = each("edge3_done", 2), each("weight3_ready", 2)
        self.out3_done, self.sum3_done, self.out3_read = new("out3_done"), new("sum3_done"), new("out3_read")
        self.out_stored = new("out_stored")
        self.ln = {s: NormSignals(new, s) for s in "TCDF"}

    def freed(self):
        return {"A_xT": self.xT_ready, "A_adjT": self.adjT_ready, "A_rows": self.rows_read, "A_E": self.E_ready,
                "C_agg": self.agg1_ready, "C_h": self.hid1_ready, "C_y": self.ln["C"].y,
                "D_agg": self.agg2_ready, "D_h0": self.hid2_ready[0], "D_h1": self.hid2_ready[1],
                "D_t0": self.silT_ready[0], "D_t1": self.silT_ready[1], "D_y": self.ln["D"].y,
                "E_xT": self.x3T_ready, "E_rows": self.rows3_read, "E_E": self.E3_ready,
                "F_V": self.V3_ready, "F_O": self.out3_read}


class NormSignals:

    def __init__(self, new, s):
        self.y, self.stats, self.mv = new(f"y_{s}"), new(f"stats_{s}"), new(f"mv_{s}")
        self.ve, self.rstd, self.norm = new(f"ve_{s}"), new(f"rstd_{s}"), new(f"norm_{s}")


class Iteration:

    def __init__(self, eng, graphs, number=None, loop=None):
        self.eng, self.graphs, self.number = eng, graphs, number
        self.base, self.kept = loop, {}

    def second(self):
        it = Iteration(self.eng, self.graphs)
        it.base, it.kept, it.shift = self.base, self.kept, 1
        return it

    shift = 0

    def plus(self, c):
        if self.number is not None:
            return self.number + c
        c += self.shift
        if c not in self.kept:
            self.kept[c] = self.eng.snap(self.base + c)
            self.eng.compute_val(self.kept[c])
        return self.kept[c]

    def plus16(self, c):
        if self.number is not None:
            return 16 * (self.number + c)
        c += self.shift
        if ("16", c) not in self.kept:
            self.kept["16", c] = self.eng.snap(self.base * 16 + 16 * c)
            self.eng.compute_val(self.kept["16", c])
        return self.kept["16", c]

    def active(self, stage, back=0):
        return self.number is None or 0 <= self.number - back - SKEW[stage] < self.graphs

    def parity(self, stage):
        i = self.number if self.number is not None else self.shift
        return (i - SKEW[stage]) % 2

    def graph(self, stage):
        return self.plus(-SKEW[stage])

    def slot(self, stage):
        c = -SKEW[stage]
        if self.number is not None:
            return (self.number + c) % RING
        c += self.shift
        if ("slot", c) not in self.kept:
            self.kept["slot", c] = self.eng.snap((self.base + c) % RING)
            self.eng.compute_val(self.kept["slot", c])
        return self.kept["slot", c]

    def had(self, stage, ago):
        return self.number is None or self.number - SKEW[stage] - ago >= 0

    def done(self, stage, ago=0):
        return self.plus(1 - SKEW[stage] - ago)

    def dma_done(self, stage, ago=0):
        return self.plus16(1 - SKEW[stage] - ago)


def run_iterations(eng, graphs, body, dma_waits=()):
    first = DEPTH + 2
    for i in range(first):
        body(Iteration(eng, graphs, number=i))
    with eng.Fori(first // 2, graphs // 2) as pair:
        it = Iteration(eng, graphs, loop=pair * 2)
        for c in range(-DEPTH - 1, 3):
            it.plus(c)
        for stage, ago in dma_waits:
            for c in range(2):
                it.plus16(1 - SKEW[stage] - ago + c)
        body(it)
        body(it.second())
    for i in range(graphs, graphs + DEPTH):
        body(Iteration(eng, graphs, number=i))


def gnn_stack(nc, x, adj, fc_w, fc_b, q_w, q_b, k_w, k_b, fp_w, fp_b,
              eps1, w11, b11, w12, b12, eps2, w21, b21, rms_w, w22, b22, w3, a3, out):
    B, N, D = x.shape
    NB = N // P
    assert D == P and NB == 2 and B % 2 == 0

    with ExitStack() as ctx:
        def sb(name, shape, dt=F32):
            return ctx.enter_context(nc.sbuf_tensor(name, shape, dt))

        def two(name, shape, dt=F32):
            return [sb(f"{name}_{p}", shape, dt) for p in range(2)]

        def bank(name):
            return ctx.enter_context(nc.psum_tensor(name, [P, 512], F32))

        attn_bank = [bank(f"attn_bank{k}") for k in range(NO)]
        val_bank = [bank(f"val_bank{k}") for k in range(2)]
        mid_bank = [bank(f"mid_bank{k}") for k in range(NMID)]

        ident = sb("ident", [P, P])
        self1 = sb("self1", [P, P])
        self2 = sb("self2", [P, P])
        minus_half = sb("minus_half", [P, 2])
        Wp = sb("Wp", [P, H0 * P])
        Wqk = sb("Wqk", [P, 2, H0])
        qk_const = sb("qk_const", [H0, 1])
        bias0 = sb("bias0", [P, P])
        W11 = sb("W11", [P, HID1])
        B11 = sb("B11", [P, HID1 // P])
        W12 = sb("W12", [P, HID1 // P, P])
        B12 = sb("B12", [P, P])
        W21 = sb("W21", [P, HID2])
        B21 = sb("B21", [P, HID2])
        RMSW = sb("RMSW", [P, HID2])
        W22 = sb("W22", [P, HID2 // P, P])
        B22 = sb("B22", [P, P])
        W3 = sb("W3", [P, P])
        Wqk3 = sb("Wqk3", [P, 2, H3])

        adjT = sb("adjT", [P, RING, NB, N], F16)
        limit = sb("limit", [P, RING, NB, N], BF16)

        x_in = two("x_in", [P, NB, P])
        adj_in = two("adj_in", [P, NB, N])
        xT = two("xT", [P, N])
        row_in = sb("row_in", [H0, 2, N])
        row_exp = sb("row_exp", [H0, 2, N])
        row_R = two("row_R", [H0, N])
        kmax = sb("kmax", [H0, 2])
        E = two("E", [P, NB, 2, H0])
        R = two("R", [P, H0, N])
        G = two("G", [P, NB, H0, GV])
        Wt = two("Wt", [P, NB, H0, N])
        x_bias = two("x_bias", [P, NB, P])
        x_half = two("x_half", [P, NB, P])
        rden = sb("rden", [P, NB, H0])
        T = two("T", [P, NB, H0, P])
        tree = sb("tree", [P, NB, 4, P])
        tree2 = sb("tree2", [P, NB, 2, P])
        tree3 = sb("tree3", [P, NB, P])
        zsum = sb("zsum", [P, NB, P])
        sg0 = sb("sg0", [P, NB, P])
        y = {s: sb(f"y_{s}", [P, NB, P]) for s in "TCDF"}
        stats = {s: sb(f"stats_{s}", [P, NB, 6]) for s in "TCDF"}
        mv = {s: sb(f"mv_{s}", [P, NB, 2]) for s in "TCDF"}
        ve = {s: sb(f"ve_{s}", [P, NB]) for s in "TCDF"}
        rstd = {s: sb(f"rstd_{s}", [P, NB]) for s in "TCDF"}
        x1 = sb("x1", [P, NB, P])
        x1_hi, x1_lo = sb("x1_hi", [P, NB, P], F16), sb("x1_lo", [P, NB, P], F16)
        x1b = sb("x1b", [P, NB, P])
        agg1T = sb("agg1T", [P, N])
        hid1T = sb("hid1T", [P, HID1 // P, N])
        x2 = sb("x2", [P, NB, P])
        x2_hi, x2_lo = sb("x2_hi", [P, NB, P], F16), sb("x2_lo", [P, NB, P], F16)
        x2b = sb("x2b", [P, NB, P])
        agg2T = sb("agg2T", [P, N])
        hid2 = sb("hid2", [P, NB, HID2])
        sumsq = sb("sumsq", [P, NB])
        msq = sb("msq", [P, NB])
        rms = sb("rms", [P, NB])
        half_rms = sb("half_rms", [P, NB])
        gate = sb("gate", [P, NB, HID2])
        tanh2 = sb("tanh2", [P, NB, HID2])
        silT = sb("silT", [P, NB, HID2 // P, P])
        x3 = two("x3", [P, NB, P])
        x3T = two("x3T", [P, N])
        row3_in = sb("row3_in", [H3, 2, N])
        row3_exp = sb("row3_exp", [H3, 2, N])
        row3_R = two("row3_R", [H3, N])
        kmax3 = sb("kmax3", [H3, 2])
        E3 = two("E3", [P, NB, 2, H3])
        R3 = two("R3", [P, H3, N])
        V3 = sb("V3", [P, NB, H3, D3 + 1])
        Wt3 = sb("Wt3", [P, NB, H3, N])
        rden3 = sb("rden3", [P, NB, H3])
        out3 = sb("out3", [P, NB, P])
        x4 = two("x4", [P, NB, P])

        R_dram = nc.dram_tensor("R_dram", [2, H0, N], F32, kind="Internal").ap()
        R3_dram = nc.dram_tensor("R3_dram", [2, H3, N], F32, kind="Internal").ap()


        fcw = Wt[0][:, 0, 0:4, :].rearrange("p a n -> p (a n)")
        fpw = Wt[0][:, 0, 4:8, :].rearrange("p a (b e) -> p (a b) e", e=P)
        fcb = sb("fcb", [P, H0])
        qkw = sb("qkw", [P, 2])
        qkb = sb("qkb", [P, 2])
        fpb = sb("fpb", [P, P])
        eps = sb("eps", [P, 2])
        acol = sb("acol", [P, 2])
        ablk = sb("ablk", [P, 2, H3])
        fcwT = Wt[0][:, 1, 0:4, :].rearrange("p a (b e) -> p (a b) e", e=P)
        w3T = sb("w3T", [P, P])
        qk_sum = sb("qk_sum", [H0, 2])

        sig = Signals(lambda name: ctx.enter_context(nc.semaphore(name)))
        freed = sig.freed()
        ln = sig.ln
        LOADS = 21

        with nc.Block() as block:
            @block.sync
            def _(sp):
                def load(dst, src):
                    sp.dma_start(dst, src).then_inc(sig.weights_loaded, 16)

                load(fcw[:, :], fc_w)
                load(fpw[:, :, :], fp_w.rearrange("(h j) e -> j h e", j=P))
                load(fcb[:, :], fc_b)
                load(qkw[:, 0:1], q_w)
                load(qkw[:, 1:2], k_w)
                load(qkb[:, 0:1], q_b.partition_broadcast(P))
                load(qkb[:, 1:2], k_b.partition_broadcast(P))
                load(fpb[:, :], fp_b.partition_broadcast(P))
                load(eps[:, 0:1], eps1.partition_broadcast(P))
                load(eps[:, 1:2], eps2.partition_broadcast(P))
                load(W11[:, :], w11)
                load(B11[:, :], b11)
                load(W12[:, :, :], w12.rearrange("(c p) n -> p c n", p=P))
                load(B12[:, :], b12.partition_broadcast(P))
                load(W21[:, :], w21)
                load(B21[:, :], b21.partition_broadcast(P))
                load(RMSW[:, :], rms_w.partition_broadcast(P))
                load(W22[:, :, :], w22.rearrange("(c p) n -> p c n", p=P))
                load(B22[:, :], b22.partition_broadcast(P))
                load(W3[:, :], w3)
                load(acol[:, :], a3)

            @block.gpsimd
            def _(pool):
                nc.gpsimd.memset(ident[:, :], 0.0).then_inc(sig.ident_zero, 1)
                pool.wait_ge(sig.ident_zero, 1)
                nc.gpsimd.affine_select(out=ident[:, :], in_=ident[:, :], compare_op=ALU.not_equal,
                                        fill=1.0, base=0, pattern=[[-1, P]],
                                        channel_multiplier=1).then_inc(sig.ident_ready, 1)

            @block.tensor
            def _(pe):
                pe.wait_ge(sig.weights_loaded, 16 * LOADS)
                pe.wait_ge(sig.ident_ready, 1)
                for h in range(H0):
                    pe.transpose(val_bank[h // 4][:, (h % 4) * P:(h % 4 + 1) * P],
                                 fcw[:, h * P:(h + 1) * P], ident[:, :])
                pe.transpose(mid_bank[0][:, 0:P], W3[:, :], ident[:, :]).then_inc(sig.turned, 1)
                pe.wait_ge(sig.turned_read, 1)
                pe.wait_ge(sig.ablk_ready, 1)
                for h in range(H0):
                    pe.matmul(attn_bank[h // 4][:, (h % 4) * P:(h % 4 + 1) * P], fcwT[:, h, :],
                              fpw[:, h, :], start=True, stop=True)
                for h in range(H0):
                    pe.matmul(attn_bank[2][:, 2 * h:2 * h + 2], fcwT[:, h, :], qkw[:, :],
                              start=True, stop=True)
                for h in range(H0):
                    pe.matmul(val_bank[0][:, 0:P], fcb[:, h:h + 1].broadcast_to([P, P]), fpw[:, h, :],
                              start=h == 0, stop=h == H0 - 1)
                pe.matmul(val_bank[1][0:H0, 0:2], fcb[:, :], qkw[:, :], start=True, stop=True)
                pe.matmul(mid_bank[0][:, 0:2 * H3], w3T[:, :], ablk[:, :, :].rearrange("p t h -> p (t h)"),
                          start=True, stop=True).then_inc(sig.folded, 1)

            @block.scalar
            def _(act):
                act.wait_ge(sig.turned, 1)
                for half in range(2):
                    nc.scalar.copy(fcwT[:, 4 * half:4 * half + 4, :].rearrange("p h j -> p (h j)"),
                                   val_bank[half][:, :])
                nc.scalar.copy(w3T[:, :], mid_bank[0][:, 0:P]).then_inc(sig.turned_read, 1)
                act.wait_ge(sig.folded, 1)
                for half in range(2):
                    nc.scalar.copy(Wp[:, 512 * half:512 * half + 512],
                                   attn_bank[half][:, :]).then_inc(sig.constants_ready, 1)

            @block.vector
            def _(dve):
                nc.vector.memset(minus_half[:, :], -0.5)
                for p in range(2):
                    nc.vector.memset(G[p][:, :, :, P:GV], 1.0)
                nc.vector.memset(V3[:, :, :, D3:D3 + 1], 1.0)
                nc.vector.memset(ablk[:, :, :], 0.0).then_inc(sig.ablk_zero, 1)
                dve.wait_ge(sig.ablk_zero, 1)
                dve.wait_ge(sig.weights_loaded, 16 * LOADS)
                for h in range(H3):
                    last = nc.vector.tensor_copy(ablk[h * D3:(h + 1) * D3, :, h],
                                                 acol[h * D3:(h + 1) * D3, :])
                last.then_inc(sig.ablk_ready, 1)
                dve.wait_ge(sig.ident_ready, 1)
                nc.vector.scalar_tensor_tensor(out=self1[:, :], in0=ident[:, :], scalar=eps[:, 0:1],
                                               in1=ident[:, :], op0=ALU.mult, op1=ALU.add)
                nc.vector.tensor_scalar(self2[:, :], ident[:, :], eps[:, 1:2], None, ALU.mult)
                dve.wait_ge(sig.folded, 1)
                nc.vector.tensor_copy(Wqk[:, :, :].rearrange("p t h -> p h t"),
                                      attn_bank[2][:, 0:2 * H0].rearrange("p (h t) -> p h t", t=2))
                nc.vector.tensor_tensor(bias0[:, :], val_bank[0][:, 0:P], fpb[:, :], ALU.add)
                nc.vector.tensor_tensor(qk_sum[:, :], val_bank[1][0:H0, 0:2], qkb[0:H0, :],
                                        ALU.add).then_inc(sig.qk_summed, 1)
                nc.vector.tensor_copy(Wqk3[:, :, :].rearrange("p t h -> p (t h)"), mid_bank[0][:, 0:2 * H3])
                dve.wait_ge(sig.qk_summed, 1)
                nc.vector.reduce_sum(qk_const[:, :], qk_sum[:, :], AX.X).then_inc(sig.constants_ready, 1)

        with nc.Block() as block:
            @block.sync
            def _(sp):
                def load(it):
                    g, p = it.graph("A"), it.parity("A")
                    if it.had("A", 2):
                        sp.wait_ge(sig.xT_done, it.done("A", 2))
                    if it.had("A", 2):
                        sp.wait_ge(sig.xbias_ready, it.done("A", 2))
                    sp.dma_start(x_in[p][:, :, :],
                                 x[g].rearrange("(b p) d -> p b d", p=P)).then_inc(sig.x_loaded, 16)
                    if it.had("A", 2):
                        sp.wait_ge(sig.adjT_done, it.done("A", 2))
                    sp.dma_start(adj_in[p][:, :, :],
                                 adj[g].rearrange("(b p) m -> p b m", p=P)).then_inc(sig.adj_loaded, 16)

                def spread(it, stage, rows, dram, wide, ready, stored, loaded, used):
                    p = it.parity(stage)
                    sp.wait_ge(ready, it.done(stage))
                    sp.dma_start(dram[p], rows[p][:, :]).then_inc(stored, 16)
                    sp.wait_ge(stored, it.dma_done(stage))
                    if it.had(stage, 2):
                        sp.wait_ge(used, it.done(stage, 2))
                    sp.dma_start(wide[p][:, :, :], dram[p].partition_broadcast(P)).then_inc(loaded, 16)

                def store(it):
                    g, p = it.graph("F"), it.parity("F")
                    sp.wait_ge(ln["F"].norm, it.done("F"))
                    sp.dma_start(out[g].rearrange("(b p) d -> p b d", p=P),
                                 x4[p][:, :, :]).then_inc(sig.out_stored, 16)

                def body(it):
                    if it.active("A"):
                        load(it)
                    if it.active("E"):
                        spread(it, "E", row3_R, R3_dram, R3, sig.rowR3_ready, sig.R3_stored,
                               sig.R3_loaded, sig.edge3_done[1])
                    if it.active("A"):
                        spread(it, "A", row_R, R_dram, R, sig.rowR_ready, sig.R_stored,
                               sig.R_loaded, sig.edge_done[3])
                    if it.active("F"):
                        store(it)

                run_iterations(sp, B, body, [("A", 0), ("E", 0)])
                sp.wait_ge(sig.out_stored, 16 * B)
                sp.wait_ge(sig.R_loaded, 16 * B)
                sp.wait_ge(sig.R3_loaded, 16 * B)

            @block.tensor
            def _(pe):
                def mid(it, name):
                    k = INDEX[name]
                    back, j = 0, k
                    while it.number is None or back <= it.number:
                        j -= NMID
                        if j < 0:
                            j, back = j + len(PHASES), back + 1
                        if it.active(PHASES[j][1], back):
                            if it.had(PHASES[j][1], back):
                                pe.wait_ge(freed[PHASES[j][0]], it.done(PHASES[j][1], back))
                            break
                    return mid_bank[k % NMID]

                def turn_x(it, name, src, written, value, done):
                    bank = mid(it, name)
                    pe.wait_ge(written, value)
                    for b in range(NB):
                        mm = pe.transpose(bank[:, b * P:(b + 1) * P], src[:, b, :], ident[:, :])
                    mm.then_inc(done, 1)

                def turn_adj(it):
                    bank, p = mid(it, "A_adjT"), it.parity("A")
                    pe.wait_ge(sig.adj_loaded, it.dma_done("A"))
                    for m in range(NB):
                        for n in range(NB):
                            mm = pe.transpose(bank[:, m * N + n * P:m * N + (n + 1) * P],
                                              adj_in[p][:, n, m * P:(m + 1) * P], ident[:, :])
                    mm.then_inc(sig.adjT_done, 1)

                def values(it, c):
                    m, half, p = c % 2, c // 2, it.parity("B")
                    if c == 0:
                        pe.wait_ge(sig.xT_ready, it.done("B"))
                    if c < 2:
                        if it.had("B", 1):
                            pe.wait_ge(sig.val_ready[c + 2], it.done("B", 1))
                    else:
                        pe.wait_ge(sig.val_ready[c - 2], it.done("B"))
                    pe.matmul(val_bank[c % 2][:, :], xT[p][:, m * P:(m + 1) * P],
                              Wp[:, 512 * half:512 * half + 512], start=True, stop=True).then_inc(sig.val_done[c], 1)

                def rows(it, name, stage, turned, w, heads, ready, done):
                    bank, p = mid(it, name), it.parity(stage)
                    pe.wait_ge(ready, it.done(stage))
                    for t in range(2):
                        mm = pe.matmul(bank[0:heads, t * N:(t + 1) * N], w[:, t, :], turned[p][:, :],
                                       start=True, stop=True)
                    mm.then_inc(done, 1)

                def turn_E(it, name, stage, src, heads, ready, done):
                    pe.wait_ge(sig.constants_ready, 3)
                    bank = mid(it, name)
                    pe.wait_ge(ready, it.done(stage))
                    for b in range(NB):
                        for t in range(2):
                            k = (b * 2 + t) * heads
                            mm = pe.transpose(bank[:, k:k + heads], src[:, t, b * P:(b + 1) * P],
                                              ident[0:heads, 0:heads])
                    mm.then_inc(done, 1)

                def attend(it, u):
                    (g, n), p = UNITS[u], it.parity("P")
                    if u == 0:
                        for c in range(2):
                            pe.wait_ge(sig.weight_ready[c], it.done("P"))
                            pe.wait_ge(sig.val_ready[c], it.done("P"))
                    if u == 2:
                        for c in range(2, 4):
                            pe.wait_ge(sig.weight_ready[c], it.done("P"))
                            pe.wait_ge(sig.val_ready[c], it.done("P"))
                    if u < NO:
                        if it.had("P", 1):
                            pe.wait_ge(sig.attn_read[u + NO], it.done("P", 1))
                    else:
                        pe.wait_ge(sig.attn_read[u - NO], it.done("P"))
                    for h in range(*GROUPS[g]):
                        k = (h - GROUPS[g][0]) * GV
                        for m in range(NB):
                            mm = pe.matmul(attn_bank[u % NO][:, k:k + GV], Wt[p][:, m, h, n * P:(n + 1) * P],
                                           G[p][:, m, h, :], start=m == 0, stop=m == NB - 1)
                    mm.then_inc(sig.attn_done[u], 1)

                def aggregate(it, name, stage, xf, hi, lo, own, norm, split, done):
                    bank, g = mid(it, name), it.slot(stage)
                    pe.wait_ge(norm, it.done(stage))
                    pe.wait_ge(split, it.done(stage))
                    for k, part in enumerate((hi, lo)):
                        for m in range(NB):
                            pe.matmul(bank[:, 0:N], part[:, m, :], adjT[:, g, m, :],
                                      start=k == 0 and m == 0, stop=False)
                    for b in range(NB):
                        mm = pe.matmul(bank[:, b * P:(b + 1) * P], xf[:, b, :], own[:, :],
                                       start=False, stop=b == NB - 1)
                    mm.then_inc(done, 1)

                def hidden1(it):
                    bank = mid(it, "C_h")
                    pe.wait_ge(sig.agg1_ready, it.done("C"))
                    for j in range(HID1 // P):
                        mm = pe.matmul(bank[:, j * N:(j + 1) * N], W11[:, j * P:(j + 1) * P], agg1T[:, :],
                                       start=True, stop=True)
                    mm.then_inc(sig.hid1_done, 1)

                def project1(it):
                    bank = mid(it, "C_y")
                    pe.wait_ge(sig.hid1_ready, it.done("C"))
                    for b in range(NB):
                        for j in range(HID1 // P):
                            mm = pe.matmul(bank[:, b * P:(b + 1) * P], hid1T[:, j, b * P:(b + 1) * P],
                                           W12[:, j, :], start=j == 0, stop=j == HID1 // P - 1)
                    mm.then_inc(sig.y1_done, 1)

                def hidden2(it, b):
                    bank = mid(it, f"D_h{b}")
                    pe.wait_ge(sig.agg2_ready, it.done("D"))
                    pe.matmul(bank[:, :], agg2T[:, b * P:(b + 1) * P], W21[:, :],
                              start=True, stop=True).then_inc(sig.hid2_done[b], 1)

                def turn_sil(it, b):
                    bank = mid(it, f"D_t{b}")
                    pe.wait_ge(sig.sil_done[b], it.done("D"))
                    for j in range(HID2 // P):
                        mm = pe.transpose(bank[:, j * P:(j + 1) * P], tanh2[:, b, j * P:(j + 1) * P], ident[:, :])
                    mm.then_inc(sig.silT_done[b], 1)

                def project2(it):
                    bank = mid(it, "D_y")
                    for b in range(NB):
                        pe.wait_ge(sig.silT_ready[b], it.done("D"))
                        for j in range(HID2 // P):
                            mm = pe.matmul(bank[:, b * P:(b + 1) * P], silT[:, b, j, :], W22[:, j, :],
                                           start=j == 0, stop=j == HID2 // P - 1)
                    mm.then_inc(sig.y2_done, 1)

                def values3(it):
                    bank, p = mid(it, "F_V"), it.parity("F")
                    pe.wait_ge(sig.x3T_ready, it.done("F"))
                    for m in range(NB):
                        mm = pe.matmul(bank[:, m * P:(m + 1) * P], x3T[p][:, m * P:(m + 1) * P], W3[:, :],
                                       start=True, stop=True)
                    mm.then_inc(sig.V3_done, 1)

                def attend3(it):
                    bank = mid(it, "F_O")
                    pe.wait_ge(sig.V3_ready, it.done("F"))
                    for m in range(NB):
                        pe.wait_ge(sig.weight3_ready[m], it.done("F"))
                    for n in range(NB):
                        for h in range(H3):
                            k = (n * H3 + h) * (D3 + 1)
                            for m in range(NB):
                                mm = pe.matmul(bank[:, k:k + D3 + 1], Wt3[:, m, h, n * P:(n + 1) * P],
                                               V3[:, m, h, :], start=m == 0, stop=m == NB - 1)
                    mm.then_inc(sig.out3_done, 1)

                def body(it):
                    a, b, p, c, d, e, f = (it.active(s) for s in "ABPCDEF")
                    if a:
                        turn_x(it, "A_xT", x_in[it.parity("A")],
                               sig.x_loaded, it.dma_done("A"), sig.xT_done)
                        turn_adj(it)
                    if b:
                        values(it, 0)
                    if d:
                        aggregate(it, "D_agg", "D", x2, x2_hi, x2_lo, self2, ln["C"].norm, sig.x2_split,
                                  sig.agg2_done)
                    if p:
                        attend(it, 0)
                    if d:
                        hidden2(it, 0)
                    if e:
                        turn_x(it, "E_xT", x3[it.parity("E")],
                               ln["D"].norm, it.done("E"), sig.x3T_done)
                    if p:
                        attend(it, 1)
                    if d:
                        hidden2(it, 1)
                    if f:
                        values3(it)
                    if a:
                        rows(it, "A_rows", "A", xT, Wqk, H0, sig.xT_ready, sig.rows_done)
                    if b:
                        values(it, 1)
                    if c:
                        aggregate(it, "C_agg", "C", x1, x1_hi, x1_lo, self1, ln["T"].norm, sig.x1_split,
                                  sig.agg1_done)
                    if e:
                        rows(it, "E_rows", "E", x3T, Wqk3, H3, sig.x3T_ready, sig.rows3_done)
                    if p:
                        attend(it, 2)
                    if f:
                        attend3(it)
                    if d:
                        turn_sil(it, 0)
                    if c:
                        hidden1(it)
                    if a:
                        turn_E(it, "A_E", "A", row_exp, H0, sig.rowE_ready, sig.E_done)
                    if p:
                        attend(it, 3)
                    if d:
                        turn_sil(it, 1)
                    if b:
                        values(it, 2)
                    if e:
                        turn_E(it, "E_E", "E", row3_exp, H3, sig.rowE3_ready, sig.E3_done)
                    if p:
                        attend(it, 4)
                    if c:
                        project1(it)
                    if b:
                        values(it, 3)
                    if d:
                        project2(it)
                    if p:
                        attend(it, 5)

                run_iterations(pe, B, body, [("A", 0)])

            @block.scalar
            def _(act):
                def copy_out(it, stage, done, dst, src, ready):
                    act.wait_ge(done, it.done(stage))
                    nc.scalar.copy(dst, src).then_inc(ready, 1)

                def bank(name):
                    return mid_bank[INDEX[name] % NMID]

                def values(it, c):
                    m, half, p = c % 2, c // 2, it.parity("B")
                    act.wait_ge(sig.val_done[c], it.done("B"))
                    nc.scalar.copy(G[p][:, m, 4 * half:4 * half + 4, 0:P],
                                   val_bank[c % 2][:, :].rearrange("p (h e) -> p h e", e=P)
                                   ).then_inc(sig.val_ready[c], 1)

                def exponentials(it, stage, slope, row, row_R, row_E, read, stored, ready, E_ready):
                    p = it.parity(stage)
                    act.wait_ge(read, it.done(stage))
                    if it.had(stage, 2):
                        act.wait_ge(stored, it.dma_done(stage, 2))
                    nc.scalar.activation(row_R[p][:, :], row[:, 0, :], ACT.Exp, scale=1.0 - slope).then_inc(ready, 1)
                    nc.scalar.activation(row_E[:, 0, :], row[:, 1, :], ACT.Exp)
                    nc.scalar.activation(row_E[:, 1, :], row[:, 1, :], ACT.Exp, scale=slope).then_inc(E_ready, 1)

                def relu1(it):
                    act.wait_ge(sig.hid1_done, it.done("C"))
                    for j in range(HID1 // P):
                        last = nc.scalar.activation(hid1T[:, j, :], bank("C_h")[:, j * N:(j + 1) * N],
                                                    ACT.Relu, bias=B11[:, j:j + 1])
                    last.then_inc(sig.hid1_ready, 1)

                def squares(it, b):
                    act.wait_ge(sig.hid2_ready[b], it.done("D"))
                    nc.scalar.activation(tanh2[:, b, :], hid2[:, b, :], ACT.Square,
                                         accum_out=sumsq[:, b:b + 1]).then_inc(sig.sumsq_done[b], 1)

                def tanhs(it, b):
                    act.wait_ge(sig.half_done, it.done("D"))
                    act.wait_ge(sig.gate_done[b], it.done("D"))
                    nc.scalar.activation(tanh2[:, b, :], gate[:, b, :], ACT.Tanh,
                                         scale=half_rms[:, b:b + 1]).then_inc(sig.tanh_done[b], 1)

                def tanh0(it):
                    act.wait_ge(sig.zsum_ready, it.done("C"))
                    nc.scalar.activation(sg0[:, :, :], zsum[:, :, :], ACT.Tanh, scale=0.5).then_inc(sig.sg0_ready, 1)

                def body(it):
                    a, b, p, c, d, e, f = (it.active(s) for s in "ABPCDEF")
                    if a:
                        copy_out(it, "A", sig.xT_done, xT[it.parity("A")][:, :], bank("A_xT")[:, 0:N], sig.xT_ready)
                        copy_out(it, "A", sig.adjT_done,
                                 adjT[:, it.slot("A"), :, :],
                                 bank("A_adjT")[:, :].rearrange("p (m n) -> p m n", m=NB), sig.adjT_ready)
                    if b:
                        values(it, 0)
                    if d:
                        copy_out(it, "D", sig.agg2_done, agg2T[:, :], bank("D_agg")[:, 0:N], sig.agg2_ready)
                    if e:
                        copy_out(it, "E", sig.x3T_done, x3T[it.parity("E")][:, :], bank("E_xT")[:, 0:N],
                                 sig.x3T_ready)
                    if c:
                        tanh0(it)
                    if d:
                        squares(it, 0)
                    if f:
                        copy_out(it, "F", sig.V3_done, V3[:, :, :, 0:D3],
                                 bank("F_V")[:, 0:N].rearrange("p (m h e) -> p m h e", m=NB, h=H3), sig.V3_ready)
                    if d:
                        squares(it, 1)
                    if b:
                        values(it, 1)
                    if a:
                        exponentials(it, "A", A0, row_in, row_R, row_exp, sig.rows_read, sig.R_stored,
                                     sig.rowR_ready, sig.rowE_ready)
                    if d:
                        tanhs(it, 0)
                    if c:
                        copy_out(it, "C", sig.agg1_done, agg1T[:, :], bank("C_agg")[:, 0:N], sig.agg1_ready)
                    if e:
                        exponentials(it, "E", A3, row3_in, row3_R, row3_exp, sig.rows3_read, sig.R3_stored,
                                     sig.rowR3_ready, sig.rowE3_ready)
                    if d:
                        tanhs(it, 1)
                        copy_out(it, "D", sig.silT_done[0], silT[:, 0, :, :].rearrange("p j n -> p (j n)"),
                                 bank("D_t0")[:, :], sig.silT_ready[0])
                    if c:
                        relu1(it)
                    if a:
                        copy_out(it, "A", sig.E_done,
                                 E[it.parity("A")][:, :, :, :].rearrange("p b t h -> p (b t h)"),
                                 bank("A_E")[:, 0:NB * 2 * H0], sig.E_ready)
                    if d:
                        copy_out(it, "D", sig.silT_done[1], silT[:, 1, :, :].rearrange("p j n -> p (j n)"),
                                 bank("D_t1")[:, :], sig.silT_ready[1])
                    if b:
                        values(it, 2)
                    if e:
                        copy_out(it, "E", sig.E3_done,
                                 E3[it.parity("E")][:, :, :, :].rearrange("p b t h -> p (b t h)"),
                                 bank("E_E")[:, 0:NB * 2 * H3], sig.E3_ready)
                    if b:
                        values(it, 3)

                run_iterations(act, B, body, [("A", 2), ("E", 2)])

            @block.vector
            def _(dve):
                def bank(name):
                    return mid_bank[INDEX[name] % NMID]

                def limits(it):
                    g = it.slot("A")
                    dve.wait_ge(sig.adjT_ready, it.done("A"))
                    nc.vector.tensor_scalar(limit[:, g, :, :], adjT[:, g, :, :], BIG, FLOOR,
                                            ALU.mult, ALU.add).then_inc(sig.limit_ready, 1)

                def row_terms(it):
                    rows = bank("A_rows")
                    dve.wait_ge(sig.rows_done, it.done("A"))
                    nc.vector.reduce_max(kmax[:, 0:1], rows[0:H0, N:2 * N], AX.X).then_inc(sig.kmax_done, 1)
                    dve.wait_ge(sig.kmax_done, it.done("A"))
                    nc.vector.tensor_scalar(kmax[:, 1:2], kmax[:, 0:1], qk_const[:, 0:1], None,
                                            ALU.add).then_inc(sig.kq_done, 1)
                    nc.vector.tensor_scalar(row_in[:, 1, :], rows[0:H0, N:2 * N], kmax[:, 0:1], None, ALU.subtract)
                    dve.wait_ge(sig.kq_done, it.done("A"))
                    nc.vector.tensor_scalar(row_in[:, 0, :], rows[0:H0, 0:N], kmax[:, 1:2], CLAMP / (1 - A0),
                                            ALU.add, ALU.min).then_inc(sig.rows_read, 1)

                def row_terms3(it):
                    rows = bank("E_rows")
                    dve.wait_ge(sig.rows3_done, it.done("E"))
                    nc.vector.reduce_max(kmax3[:, 0:1], rows[0:H3, N:2 * N], AX.X).then_inc(sig.kmax3_done, 1)
                    dve.wait_ge(sig.kmax3_done, it.done("E"))
                    nc.vector.tensor_scalar(row3_in[:, 1, :], rows[0:H3, N:2 * N], kmax3[:, 0:1], None,
                                            ALU.subtract)
                    nc.vector.tensor_scalar(row3_in[:, 0, :], rows[0:H3, 0:N], kmax3[:, 0:1], CLAMP / (1 - A3),
                                            ALU.add, ALU.min).then_inc(sig.rows3_read, 1)

                def weights(it, c):
                    m, half, p, g = c % 2, c // 2, it.parity("B"), it.slot("B")
                    if c == 0:
                        dve.wait_ge(sig.E_ready, it.done("B"))
                        if it.had("B", 2):
                            dve.wait_ge(sig.attn_done[5], it.done("B", 2))
                        dve.wait_ge(sig.R_loaded, it.dma_done("B"))
                    hs = range(4 * half, 4 * half + 4)
                    for h in hs:
                        last = nc.vector.tensor_scalar(Wt[p][:, m, h, :], R[p][:, h, :], E[p][:, m, 0, h:h + 1],
                                                       E[p][:, m, 1, h:h + 1], ALU.mult, ALU.max)
                    last.then_inc(sig.edge_done[c], 1)
                    if c == 0:
                        dve.wait_ge(sig.limit_ready, it.done("B"))
                    dve.wait_ge(sig.edge_done[c], it.done("B"))
                    w = Wt[p][:, m, 4 * half:4 * half + 4, :]
                    nc.vector.tensor_tensor(w, w, limit[:, g, m, :].unsqueeze(1).broadcast_to([P, 4, N]),
                                            ALU.min).then_inc(sig.weight_ready[c], 1)

                def weights3(it, m):
                    p, g = it.parity("F"), it.slot("F")
                    if m == 0:
                        dve.wait_ge(sig.E3_ready, it.done("F"))
                        if it.had("F", 1):
                            dve.wait_ge(sig.out3_done, it.done("F", 1))
                        dve.wait_ge(sig.R3_loaded, it.dma_done("F"))
                    for h in range(H3):
                        last = nc.vector.tensor_scalar(Wt3[:, m, h, :], R3[p][:, h, :], E3[p][:, m, 0, h:h + 1],
                                                       E3[p][:, m, 1, h:h + 1], ALU.mult, ALU.max)
                    last.then_inc(sig.edge3_done[m], 1)
                    dve.wait_ge(sig.edge3_done[m], it.done("F"))
                    nc.vector.tensor_tensor(Wt3[:, m, :, :], Wt3[:, m, :, :],
                                            limit[:, g, m, :].unsqueeze(1).broadcast_to([P, H3, N]),
                                            ALU.min).then_inc(sig.weight3_ready[m], 1)

                def normalise(it, u):
                    (g, n), p = UNITS[u], it.parity("P")
                    lo, hi = GROUPS[g]
                    if u == 0:
                        if it.had("P", 2):
                            dve.wait_ge(sig.tree1_done, it.done("P", 2))
                    dve.wait_ge(sig.attn_done[u], it.done("P"))
                    o = attn_bank[u % NO][:, 0:(hi - lo) * GV].rearrange("p (h e) -> p h e", e=GV)
                    nc.vector.reciprocal(rden[:, n, lo:hi], o[:, :, P]).then_inc(sig.attn_sum[u], 1)
                    dve.wait_ge(sig.attn_sum[u], it.done("P"))
                    nc.vector.tensor_tensor(T[p][:, n, lo:hi, :], o[:, :, 0:P],
                                            rden[:, n, lo:hi].unsqueeze(2).broadcast_to([P, hi - lo, P]),
                                            ALU.mult).then_inc(sig.attn_read[u], 1)

                def moments(it, s, stage):
                    dve.wait_ge(ln[s].y, it.done(stage))
                    for b in range(NB):
                        last = nc.vector.bn_stats(stats[s][:, b, :], y[s][:, b, :])
                    last.then_inc(ln[s].stats, 1)
                    dve.wait_ge(sig.constants_ready, 3)
                    dve.wait_ge(ln[s].stats, it.done(stage))
                    for b in range(NB):
                        last = nc.vector.bn_aggr(mv[s][:, b, :], stats[s][:, b, :])
                    last.then_inc(ln[s].mv, 1)

                def norm(it, s, stage, dst):
                    dve.wait_ge(ln[s].rstd, it.done(stage))
                    for b in range(NB):
                        last = nc.vector.tensor_scalar(dst[:, b, :], y[s][:, b, :], mv[s][:, b, 0:1],
                                                       rstd[s][:, b:b + 1], ALU.subtract, ALU.mult)
                    last.then_inc(ln[s].norm, 1)

                def residual0(it):
                    p = it.parity("C")
                    dve.wait_ge(sig.sg0_ready, it.done("C"))
                    nc.vector.scalar_tensor_tensor(out=y["T"][:, :, :], in0=sg0[:, :, :], scalar=0.5,
                                                   in1=x_half[p][:, :, :], op0=ALU.mult,
                                                   op1=ALU.add).then_inc(ln["T"].y, 1)

                def residual1(it):
                    dve.wait_ge(sig.y1_done, it.done("C"))
                    dve.wait_ge(sig.x1b_ready, it.done("C"))
                    nc.vector.tensor_tensor(y["C"][:, :, :],
                                            bank("C_y")[:, 0:N].rearrange("p (b e) -> p b e", b=NB),
                                            x1b[:, :, :], ALU.add).then_inc(ln["C"].y, 1)

                def hidden2(it, b):
                    dve.wait_ge(sig.hid2_done[b], it.done("D"))
                    nc.vector.tensor_tensor(hid2[:, b, :], bank(f"D_h{b}")[:, :], B21[:, :],
                                            ALU.add).then_inc(sig.hid2_ready[b], 1)

                def silu2(it, b):
                    dve.wait_ge(sig.tanh_done[b], it.done("D"))
                    nc.vector.scalar_tensor_tensor(out=tanh2[:, b, :], in0=tanh2[:, b, :], scalar=1.0,
                                                   in1=gate[:, b, :], op0=ALU.add,
                                                   op1=ALU.mult).then_inc(sig.sil_done[b], 1)

                def residual2(it):
                    dve.wait_ge(sig.y2_done, it.done("D"))
                    dve.wait_ge(sig.x2b_ready, it.done("D"))
                    for b in range(NB):
                        last = nc.vector.scalar_tensor_tensor(
                            out=y["D"][:, b, :], in0=bank("D_y")[:, b * P:(b + 1) * P],
                            scalar=half_rms[:, b:b + 1], in1=x2b[:, b, :], op0=ALU.mult, op1=ALU.add)
                    last.then_inc(ln["D"].y, 1)

                def residual3(it):
                    p = it.parity("F")
                    dve.wait_ge(sig.out3_done, it.done("F"))
                    o = bank("F_O")[:, 0:NB * H3 * (D3 + 1)].rearrange("p (k e) -> p k e", e=D3 + 1)
                    nc.vector.reciprocal(rden3[:, :, :].rearrange("p b h -> p (b h)"),
                                         o[:, :, D3]).then_inc(sig.sum3_done, 1)
                    dve.wait_ge(sig.sum3_done, it.done("F"))
                    nc.vector.tensor_tensor(
                        out3[:, :, :].rearrange("p b (h e) -> p (b h) e", h=H3), o[:, :, 0:D3],
                        rden3[:, :, :].rearrange("p b h -> p (b h)").unsqueeze(2).broadcast_to([P, NB * H3, D3]),
                        ALU.mult).then_inc(sig.out3_read, 1)
                    dve.wait_ge(sig.out3_read, it.done("F"))
                    nc.vector.tensor_tensor(y["F"][:, :, :], out3[:, :, :], x3[p][:, :, :],
                                            ALU.add).then_inc(ln["F"].y, 1)

                def body(it):
                    a, b, p, c, d, e, f = (it.active(s) for s in "ABPCDEF")
                    if b:
                        weights(it, 0)
                    if a:
                        limits(it)
                    if p:
                        normalise(it, 0)
                    if c:
                        residual0(it)
                        moments(it, "T", "C")
                    if d:
                        hidden2(it, 0)
                    if p:
                        normalise(it, 1)
                    if c:
                        if it.had("C", 1):
                            dve.wait_ge(sig.agg1_done, it.done("C", 1))
                        if it.had("C", 1):
                            dve.wait_ge(sig.x1b_ready, it.done("C", 1))
                        norm(it, "T", "C", x1)
                    if d:
                        hidden2(it, 1)
                    if a:
                        row_terms(it)
                    if b:
                        weights(it, 1)
                    if f:
                        weights3(it, 0)
                        weights3(it, 1)
                    if e:
                        row_terms3(it)
                    if d:
                        silu2(it, 0)
                    if p:
                        normalise(it, 2)
                    if f:
                        residual3(it)
                        moments(it, "F", "F")
                    if d:
                        silu2(it, 1)
                    if p:
                        normalise(it, 3)
                    if f:
                        if it.had("F", 2):
                            dve.wait_ge(sig.out_stored, it.dma_done("F", 2))
                        norm(it, "F", "F", x4[it.parity("F")])
                    if b:
                        weights(it, 2)
                    if p:
                        normalise(it, 4)
                    if c:
                        residual1(it)
                        moments(it, "C", "C")
                    if b:
                        weights(it, 3)
                    if c:
                        if it.had("C", 1):
                            dve.wait_ge(sig.agg2_done, it.done("C", 1))
                        if it.had("C", 1):
                            dve.wait_ge(sig.x2b_ready, it.done("C", 1))
                        norm(it, "C", "C", x2)
                    if d:
                        residual2(it)
                        moments(it, "D", "D")
                    if p:
                        normalise(it, 5)
                    if d:
                        norm(it, "D", "D", x3[it.parity("D")])

                run_iterations(dve, B, body, [("B", 0), ("F", 0), ("F", 2)])

            @block.gpsimd
            def _(pool):
                def head_sum(it):
                    t = T[it.parity("C")]
                    pool.wait_ge(sig.attn_read[5], it.done("C"))
                    nc.gpsimd.tensor_tensor(tree[:, :, :, :], t[:, :, 0:4, :], t[:, :, 4:8, :],
                                            ALU.add).then_inc(sig.tree1_done, 1)
                    pool.wait_ge(sig.tree1_done, it.done("C"))
                    nc.gpsimd.tensor_tensor(tree2[:, :, :, :], tree[:, :, 0:2, :], tree[:, :, 2:4, :],
                                            ALU.add).then_inc(sig.tree2_done, 1)
                    pool.wait_ge(sig.tree2_done, it.done("C"))
                    nc.gpsimd.tensor_tensor(tree3[:, :, :], tree2[:, :, 0, :], tree2[:, :, 1, :],
                                            ALU.add).then_inc(sig.tree3_done, 1)
                    pool.wait_ge(sig.tree3_done, it.done("C"))
                    nc.gpsimd.tensor_tensor(zsum[:, :, :], tree3[:, :, :], x_bias[it.parity("C")][:, :, :],
                                            ALU.add).then_inc(sig.zsum_ready, 1)

                def x_terms(it):
                    p = it.parity("B")
                    pool.wait_ge(sig.constants_ready, 3)
                    if it.had("B", 2):
                        pool.wait_ge(ln["T"].y, it.done("B", 2))
                    pool.wait_ge(sig.x_loaded, it.dma_done("B"))
                    nc.gpsimd.tensor_scalar(x_half[p][:, :, :], x_in[p][:, :, :], 0.5, 1.0, ALU.add, ALU.mult)
                    nc.gpsimd.tensor_tensor(x_bias[p][:, :, :], x_in[p][:, :, :],
                                            bias0[:, :].unsqueeze(1).broadcast_to([P, NB, P]),
                                            ALU.add).then_inc(sig.xbias_ready, 1)

                def rsqrt_var(it, s, stage):
                    pool.wait_ge(sig.constants_ready, 3)
                    pool.wait_ge(ln[s].mv, it.done(stage))
                    nc.gpsimd.tensor_scalar(ve[s][:, :], mv[s][:, :, 1], LN_EPS, 1.0, ALU.add,
                                            ALU.mult).then_inc(ln[s].ve, 1)
                    pool.wait_ge(ln[s].ve, it.done(stage))
                    nc.gpsimd.tensor_tensor(rstd[s][:, :], ve[s][:, :], minus_half[:, :],
                                            ALU.pow).then_inc(ln[s].rstd, 1)

                def split(it, stage, src, hi, lo, agg_done, norm_done, hi_done, done):
                    pool.wait_ge(sig.constants_ready, 3)
                    pool.wait_ge(norm_done, it.done(stage))
                    if it.had(stage, 1):
                        pool.wait_ge(agg_done, it.done(stage, 1))
                    nc.gpsimd.tensor_copy(hi[:, :, :], src[:, :, :]).then_inc(hi_done, 1)
                    pool.wait_ge(hi_done, it.done(stage))
                    nc.gpsimd.tensor_tensor(lo[:, :, :], src[:, :, :], hi[:, :, :], ALU.subtract).then_inc(done, 1)

                def add_bias(it, stage, dst, src, bias, y_done, done):
                    if it.had(stage, 1):
                        pool.wait_ge(y_done, it.done(stage, 1))
                    nc.gpsimd.tensor_tensor(dst[:, :, :], src[:, :, :],
                                            bias[:, :].unsqueeze(1).broadcast_to([P, NB, P]),
                                            ALU.add).then_inc(done, 1)

                def gates(it, b):
                    pool.wait_ge(sig.hid2_ready[b], it.done("D"))
                    if it.had("D", 1):
                        pool.wait_ge(sig.sil_done[b], it.done("D", 1))
                    nc.gpsimd.tensor_tensor(gate[:, b, :], hid2[:, b, :], RMSW[:, :],
                                            ALU.mult).then_inc(sig.gate_done[b], 1)

                def rsqrt_rms(it):
                    pool.wait_ge(sig.constants_ready, 3)
                    if it.had("D", 1):
                        pool.wait_ge(ln["D"].y, it.done("D", 1))
                    for b in range(NB):
                        pool.wait_ge(sig.sumsq_done[b], it.done("D"))
                    nc.gpsimd.tensor_scalar(msq[:, :], sumsq[:, :], 1.0 / HID2, RMS_EPS, ALU.mult,
                                            ALU.add).then_inc(sig.msq_done, 1)
                    pool.wait_ge(sig.msq_done, it.done("D"))
                    nc.gpsimd.tensor_tensor(rms[:, :], msq[:, :], minus_half[:, :],
                                            ALU.pow).then_inc(sig.rms_done, 1)
                    pool.wait_ge(sig.constants_ready, 3)
                    pool.wait_ge(sig.rms_done, it.done("D"))
                    nc.gpsimd.tensor_scalar(half_rms[:, :], rms[:, :], 0.5, 1.0, ALU.mult,
                                            ALU.mult).then_inc(sig.half_done, 1)

                def body(it):
                    a, b, p, c, d, e, f = (it.active(s) for s in "ABPCDEF")
                    if c:
                        head_sum(it)
                    if b:
                        x_terms(it)
                    if d:
                        gates(it, 0)
                    if c:
                        rsqrt_var(it, "T", "C")
                        split(it, "C", x1, x1_hi, x1_lo, sig.agg1_done, ln["T"].norm, sig.x1_hi_done, sig.x1_split)
                        add_bias(it, "C", x1b, x1, B12, ln["C"].y, sig.x1b_ready)
                    if d:
                        gates(it, 1)
                        rsqrt_rms(it)
                        add_bias(it, "D", x2b, x2, B22, ln["D"].y, sig.x2b_ready)
                    if f:
                        rsqrt_var(it, "F", "F")
                    if c:
                        rsqrt_var(it, "C", "C")
                        split(it, "C", x2, x2_hi, x2_lo, sig.agg2_done, ln["C"].norm, sig.x2_hi_done, sig.x2_split)
                    if d:
                        rsqrt_var(it, "D", "D")

                run_iterations(pool, B, body, [("B", 0)])


_INS = ["x", "adj", "L0_gnn_fc_w", "L0_gnn_fc_b", "L0_gnn_q_w", "L0_gnn_q_b", "L0_gnn_k_w", "L0_gnn_k_b",
        "L0_gnn_fp_w", "L0_gnn_fp_b", "L1_gnn_eps", "L1_gnn_W1", "L1_gnn_b1", "L1_gnn_W2", "L1_gnn_b2",
        "L2_gnn_epsilon", "L2_gnn_W1", "L2_gnn_b1", "L2_gnn_rms_weight", "L2_gnn_W2", "L2_gnn_b2",
        "L3_gnn_W", "L3_gnn_a"]


def kernel(**inputs):
    import numpy as _np
    import concourse.bacc as _bacc
    from concourse import mybir as _mybir
    from concourse.bass_utils import run_bass_kernel_spmd as _run

    nc = _bacc.Bacc("TRN2", target_bir_lowering=False, num_devices=1)
    arrays, args = {}, []
    laid_out = {
        "L0_gnn_fc_b": lambda v: v.reshape(H0, P).T,
        "L1_gnn_b1": lambda v: v.reshape(HID1 // P, P).T,
        "L3_gnn_a": lambda v: v.reshape(H3, 2, D3).transpose(0, 2, 1).reshape(P, 2),
    }
    for name in _INS:
        a = _np.asarray(inputs[name])
        a = _np.ascontiguousarray(laid_out[name](a) if name in laid_out else a)
        a = a.reshape(a.shape or (1,))
        arrays[f"in_{name}_dram"] = a
        args.append(nc.dram_tensor(f"in_{name}_dram", a.shape, _mybir.dt.from_np(a.dtype), kind="ExternalInput").ap())
    out = nc.dram_tensor("out_dram", inputs["x"].shape, _mybir.dt.float32, kind="ExternalOutput").ap()
    gnn_stack(nc, *args, out)
    r = _run(nc, [arrays], core_ids=[0])
    return r.results[0]["out_dram"]
```

```python
from contextlib import ExitStack

import concourse.bass as bass
from concourse import mybir

ALU = mybir.AluOpType
ACT = mybir.ActivationFunctionType
AX = mybir.AxisListType
F32 = mybir.dt.float32
F16 = mybir.dt.float16
BF16 = mybir.dt.bfloat16

P = 128
H0, H3 = 8, 4
A0, A3 = 0.01, 0.2
D3 = P // H3
HID1, HID2 = 256, 512
LN_EPS, RMS_EPS = 1e-5, 1e-6
CLAMP = 60.0
BIG = 2.0 ** 127
FLOOR = 2.0 ** -80
GV = P + 1
GROUPS = ((0, 3), (3, 6), (6, 8))
UNITS = [(g, nb) for g in range(3) for nb in range(2)]
NO = 2

SKEW = dict(A=0, B=1, P=2, C=3, D=4, E=5, F=6, S=7)
DEPTH = max(SKEW.values())
RING = 8

PHASES = [
    ("A_xT", "A"), ("A_adjT", "A"), ("A_rows", "A"), ("E_xT", "E"), ("F_V", "F"),
    ("D_agg", "D"), ("D_h0", "D"), ("D_h1", "D"), ("E_rows", "E"), ("F_O0", "F"),
    ("F_O1", "F"), ("C_agg", "C"), ("D_t1", "D"), ("D_t0", "D"), ("F_T", "F"),
    ("C_h", "C"), ("A_E", "A"), ("D_y", "D"), ("C_y", "C"), ("E_E", "E"),
]
NMID = 4
ACT0 = (True, True, True, True)
ACT3 = (True, True)
KROW = 32
INDEX = {name: k for k, (name, _) in enumerate(PHASES)}


class Signals:

    def __init__(self, new):
        def each(name, n):
            return [new(f"{name}{k}") for k in range(n)]

        self.weights_loaded = new("weights_loaded")
        self.ident_zero, self.ident_ready = new("ident_zero"), new("ident_ready")
        self.turned, self.turned_read, self.folded = new("turned"), new("turned_read"), new("folded")
        self.zeroed, self.ablk_ready, self.b21_split = new("zeroed"), new("ablk_ready"), new("b21_split")
        self.qk_summed, self.constants_ready = new("qk_summed"), new("constants_ready")
        self.x_loaded, self.adj_loaded = new("x_loaded"), new("adj_loaded")
        self.xT_done, self.xT_ready = new("xT_done"), new("xT_ready")
        self.adjT_done, self.adjT_ready, self.limit_ready = new("adjT_done"), new("adjT_ready"), new("limit_ready")
        self.rows_done, self.rows_read = new("rows_done"), new("rows_read")
        self.kmax_done, self.kq_done = new("kmax_done"), new("kq_done")
        self.rowR_ready, self.rowE_ready = new("rowR_ready"), new("rowE_ready")
        self.R_stored, self.R_loaded = new("R_stored"), new("R_loaded")
        self.E_done, self.E_ready = new("E_done"), new("E_ready")
        self.val_done, self.val_ready = each("val_done", 4), each("val_ready", 4)
        self.edge_done, self.weight_ready = each("edge_done", 4), each("weight_ready", 4)
        self.xbias_ready = new("xbias_ready")
        self.attn_done, self.attn_sum, self.attn_read = each("attn_done", 6), each("attn_sum", 6), each("attn_read", 6)
        self.tree1_done, self.tree2_done, self.tree3_done = new("tree1_done"), new("tree2_done"), new("tree3_done")
        self.zsum_ready, self.sg0_ready = new("zsum_ready"), new("sg0_ready")
        self.x1_hi_done, self.x1_split, self.x1b_ready = new("x1_hi_done"), new("x1_split"), new("x1b_ready")
        self.agg1_done, self.agg1_ready = new("agg1_done"), new("agg1_ready")
        self.hid1_done, self.hid1_ready, self.y1_done = new("hid1_done"), new("hid1_ready"), new("y1_done")
        self.x2_hi_done, self.x2_split, self.x2b_ready = new("x2_hi_done"), new("x2_split"), new("x2b_ready")
        self.agg2_done, self.agg2_ready = new("agg2_done"), new("agg2_ready")
        self.hid2_done, self.hid2_ready = each("hid2_done", 2), each("hid2_ready", 2)
        self.sumsq_done, self.gate_done = each("sumsq_done", 2), each("gate_done", 2)
        self.msq_done, self.rms_done, self.half_done = new("msq_done"), new("rms_done"), new("half_done")
        self.tanh_done, self.sil_done = each("tanh_done", 2), each("sil_done", 2)
        self.silT_done, self.silT_ready = each("silT_done", 2), each("silT_ready", 2)
        self.y2_done = new("y2_done")
        self.x3T_done, self.x3T_ready = new("x3T_done"), new("x3T_ready")
        self.rows3_done, self.kmax3_done, self.rows3_read = new("rows3_done"), new("kmax3_done"), new("rows3_read")
        self.kq3_done = new("kq3_done")
        self.rowR3_ready, self.rowE3_ready = new("rowR3_ready"), new("rowE3_ready")
        self.R3_stored, self.R3_loaded = new("R3_stored"), new("R3_loaded")
        self.E3_done, self.E3_ready = new("E3_done"), new("E3_ready")
        self.V3_done, self.V3_ready = new("V3_done"), new("V3_ready")
        self.edge3_done, self.weight3_ready = each("edge3_done", 2), each("weight3_ready", 2)
        self.out3T_done, self.out3T_ready = each("out3T_done", 2), each("out3T_ready", 2)
        self.out3_done, self.sum3_done, self.out3_read = new("out3_done"), new("sum3_done"), new("out3_read")
        self.out_stored = new("out_stored")
        self.ln = {s: NormSignals(new, s) for s in "TCDF"}

    def freed(self):
        return {"A_xT": self.xT_ready, "A_adjT": self.adjT_ready, "A_rows": self.rows_read, "A_E": self.E_ready,
                "C_agg": self.agg1_ready, "C_h": self.hid1_ready, "C_y": self.ln["C"].y,
                "D_agg": self.agg2_ready, "D_h0": self.sumsq_done[0], "D_h1": self.sumsq_done[1],
                "D_t0": self.silT_ready[0], "D_t1": self.silT_ready[1], "D_y": self.ln["D"].y,
                "E_xT": self.x3T_ready, "E_rows": self.rows3_read, "E_E": self.E3_ready,
                "F_V": self.V3_ready, "F_O0": self.out3T_ready[0], "F_O1": self.out3T_ready[1],
                "F_T": self.out3_read}


class NormSignals:

    def __init__(self, new, s):
        self.y, self.stats, self.mv = new(f"y_{s}"), new(f"stats_{s}"), new(f"mv_{s}")
        self.ve, self.rstd, self.norm = new(f"ve_{s}"), new(f"rstd_{s}"), new(f"norm_{s}")


class Iteration:

    def __init__(self, eng, graphs, number=None, loop=None):
        self.eng, self.graphs, self.number = eng, graphs, number
        self.base, self.kept = loop, {}

    def second(self):
        it = Iteration(self.eng, self.graphs)
        it.base, it.kept, it.shift = self.base, self.kept, 1
        return it

    shift = 0

    def plus(self, c):
        if self.number is not None:
            return self.number + c
        c += self.shift
        if c not in self.kept:
            self.kept[c] = self.eng.snap(self.base + c)
            self.eng.compute_val(self.kept[c])
        return self.kept[c]

    def plus16(self, c):
        if self.number is not None:
            return 16 * (self.number + c)
        c += self.shift
        if ("16", c) not in self.kept:
            self.kept["16", c] = self.eng.snap(self.base * 16 + 16 * c)
            self.eng.compute_val(self.kept["16", c])
        return self.kept["16", c]

    def active(self, stage, back=0):
        return self.number is None or 0 <= self.number - back - SKEW[stage] < self.graphs

    def parity(self, stage):
        i = self.number if self.number is not None else self.shift
        return (i - SKEW[stage]) % 2

    def graph(self, stage):
        return self.plus(-SKEW[stage])

    def slot(self, stage):
        c = -SKEW[stage]
        if self.number is not None:
            return (self.number + c) % RING
        c += self.shift
        if ("slot", c) not in self.kept:
            self.kept["slot", c] = self.eng.snap((self.base + c) % RING)
            self.eng.compute_val(self.kept["slot", c])
        return self.kept["slot", c]

    def had(self, stage, ago):
        return self.number is None or self.number - SKEW[stage] - ago >= 0

    def done(self, stage, ago=0):
        return self.plus(1 - SKEW[stage] - ago)

    def dma_done(self, stage, ago=0):
        return self.plus16(1 - SKEW[stage] - ago)


def run_iterations(eng, graphs, body, dma_waits=()):
    first = SKEW["F"] + 2
    for i in range(first):
        body(Iteration(eng, graphs, number=i))
    with eng.Fori(first // 2, graphs // 2) as pair:
        it = Iteration(eng, graphs, loop=pair * 2)
        for c in range(-DEPTH - 1, 3):
            it.plus(c)
        for stage, ago in dma_waits:
            for c in range(2):
                it.plus16(1 - SKEW[stage] - ago + c)
        body(it)
        body(it.second())
    for i in range(graphs, graphs + DEPTH):
        body(Iteration(eng, graphs, number=i))


def gnn_stack(nc, x, adj, fc_w, fc_b, q_w, q_b, k_w, k_b, fp_w, fp_b,
              eps1, w11, b11, w12, b12, eps2, w21, b21, rms_w, w22, b22, w3, a3, out):
    B, N, D = x.shape
    NB = N // P
    assert D == P and NB == 2 and B % 2 == 0

    with ExitStack() as ctx:
        def sb(name, shape, dt=F32):
            return ctx.enter_context(nc.sbuf_tensor(name, shape, dt))

        def two(name, shape, dt=F32):
            return [sb(f"{name}_{p}", shape, dt) for p in range(2)]

        def bank(name):
            return ctx.enter_context(nc.psum_tensor(name, [P, 512], F32))

        attn_bank = [bank(f"attn_bank{k}") for k in range(NO)]
        val_bank = [bank(f"val_bank{k}") for k in range(2)]
        mid_bank = [bank(f"mid_bank{k}") for k in range(NMID)]

        ident = sb("ident", [P, P])
        self1 = sb("self1", [P, P])
        self2 = sb("self2", [P, P])
        minus_half = sb("minus_half", [P, 2])
        Wp = sb("Wp", [P, H0 * P])
        Wqk = sb("Wqk", [P, KROW + H0])
        qk_const = sb("qk_const", [KROW + H0, 1])
        bias0 = sb("bias0", [P, P])
        W11 = sb("W11", [P, HID1])
        B11 = sb("B11", [P, HID1 // P])
        W12 = sb("W12", [P, HID1 // P, P])
        B12 = sb("B12", [P, P])
        W21 = sb("W21", [P, HID2])
        B21 = sb("B21", [2 * KROW + 1, HID2], BF16)
        ones = sb("ones", [2 * KROW + 1, P], BF16)
        RMSW = sb("RMSW", [P, HID2])
        W22 = sb("W22", [P, HID2 // P, P])
        B22 = sb("B22", [P, P])
        W3 = sb("W3", [P, P])
        Wqk3 = sb("Wqk3", [P, KROW + H3])

        adjT = sb("adjT", [P, RING, NB, N], F16)
        limit = sb("limit", [P, RING, NB, N], BF16)

        x_in = two("x_in", [P, NB, P])
        adj_in = two("adj_in", [P, NB, N])
        xT = two("xT", [P, N])
        row_in = sb("row_in", [H0, 2, N])
        row_exp = sb("row_exp", [H0, 2, N])
        row_R = two("row_R", [H0, N])
        kmax = sb("kmax", [KROW + H0, 1])
        kq = sb("kq", [H0, 1])
        E = two("E", [P, NB, 2, H0])
        nE = two("nE", [P, NB, H0])
        R = two("R", [P, H0, N])
        G = two("G", [P, NB, H0, GV])
        Wt = two("Wt", [P, NB, H0, N])
        x_bias = two("x_bias", [P, NB, P])
        x_half = two("x_half", [P, NB, P])
        rden = sb("rden", [P, NB, H0])
        T = two("T", [P, NB, H0, P])
        zsum = sb("zsum", [P, NB, P])
        sg0 = sb("sg0", [P, NB, P])
        y = {s: sb(f"y_{s}", [P, NB, P]) for s in "TCDF"}
        stats = {s: sb(f"stats_{s}", [P, NB, 6]) for s in "TCDF"}
        mv = {s: sb(f"mv_{s}", [P, NB, 2]) for s in "TCDF"}
        ve = {s: sb(f"ve_{s}", [P, NB]) for s in "TCDF"}
        rstd = {s: sb(f"rstd_{s}", [P, NB]) for s in "TCDF"}
        x1 = sb("x1", [P, NB, P])
        x1_hi, x1_lo = sb("x1_hi", [P, NB, P], F16), sb("x1_lo", [P, NB, P], F16)
        x1b = sb("x1b", [P, NB, P])
        agg1T = sb("agg1T", [P, N])
        hid1T = sb("hid1T", [P, HID1 // P, N])
        x2 = sb("x2", [P, NB, P])
        x2_hi, x2_lo = sb("x2_hi", [P, NB, P], F16), sb("x2_lo", [P, NB, P], F16)
        x2b = sb("x2b", [P, NB, P])
        agg2T = sb("agg2T", [P, N])
        hid2 = sb("hid2", [P, NB, HID2])
        sumsq = sb("sumsq", [P, NB])
        msq = sb("msq", [P, NB])
        rms = sb("rms", [P, NB])
        half_rms = sb("half_rms", [P, NB])
        gate = sb("gate", [P, NB, HID2])
        tanh2 = sb("tanh2", [P, NB, HID2])
        silT = sb("silT", [P, NB, HID2 // P, P])
        x3 = two("x3", [P, NB, P])
        x3T = two("x3T", [P, N])
        row3_in = sb("row3_in", [H3, 2, N])
        row3_exp = sb("row3_exp", [H3, 2, N])
        row3_R = two("row3_R", [H3, N])
        kmax3 = sb("kmax3", [KROW + H3, 1])
        kq3 = sb("kq3", [H3, 1])
        E3 = two("E3", [P, NB, 2, H3])
        nE3 = two("nE3", [P, NB, H3])
        R3 = two("R3", [P, H3, N])
        V3 = sb("V3", [P, NB, H3, D3 + 1])
        Wt3 = sb("Wt3", [P, NB, H3, N])
        rden3 = sb("rden3", [P, NB, H3])
        out3T = sb("out3T", [D3 + 1, 2, 2 * N])
        out3 = sb("out3", [P, NB, P])
        x4 = two("x4", [P, NB, P])

        R_dram = nc.dram_tensor("R_dram", [2, H0, N], F32, kind="Internal").ap()
        R3_dram = nc.dram_tensor("R3_dram", [2, H3, N], F32, kind="Internal").ap()


        fcw = Wt[0][:, 0, 0:4, :].rearrange("p a n -> p (a n)")
        fpw = Wt[0][:, 0, 4:8, :].rearrange("p a (b e) -> p (a b) e", e=P)
        fcb = sb("fcb", [P, H0])
        qkw = sb("qkw", [P, 2])
        qkb = sb("qkb", [P, 2])
        fpb = sb("fpb", [P, P])
        eps = sb("eps", [P, 2])
        acol = sb("acol", [P, 2])
        ablk = sb("ablk", [P, 2, H3])
        fcwT = Wt[0][:, 1, 0:4, :].rearrange("p a (b e) -> p (a b) e", e=P)
        w3T = sb("w3T", [P, P])
        qk_sum = sb("qk_sum", [KROW + H0, 2])
        b21row = sb("b21row", [1, 2, HID2])
        low = sb("low", [1, HID2], BF16)

        sig = Signals(lambda name: ctx.enter_context(nc.semaphore(name)))
        freed = sig.freed()
        ln = sig.ln
        LOADS = 21

        with nc.Block() as block:
            @block.sync
            def _(sp):
                def load(dst, src):
                    sp.dma_start(dst, src).then_inc(sig.weights_loaded, 16)

                load(fcw[:, :], fc_w)
                load(fpw[:, :, :], fp_w.rearrange("(h j) e -> j h e", j=P))
                load(fcb[:, :], fc_b)
                load(qkw[:, 0:1], q_w)
                load(qkw[:, 1:2], k_w)
                load(qkb[:, 0:1], q_b.partition_broadcast(P))
                load(qkb[:, 1:2], k_b.partition_broadcast(P))
                load(fpb[:, :], fp_b.partition_broadcast(P))
                load(eps[:, 0:1], eps1.partition_broadcast(P))
                load(eps[:, 1:2], eps2.partition_broadcast(P))
                load(W11[:, :], w11)
                load(B11[:, :], b11)
                load(W12[:, :, :], w12.rearrange("(c p) n -> p c n", p=P))
                load(B12[:, :], b12.partition_broadcast(P))
                load(W21[:, :], w21)
                load(b21row[:, 0, :], b21.partition_broadcast(1))
                load(RMSW[:, :], rms_w.partition_broadcast(P))
                load(W22[:, :, :], w22.rearrange("(c p) n -> p c n", p=P))
                load(B22[:, :], b22.partition_broadcast(P))
                load(W3[:, :], w3)
                load(acol[:, :], a3)

            @block.gpsimd
            def _(pool):
                nc.gpsimd.memset(ident[:, :], 0.0).then_inc(sig.ident_zero, 1)
                pool.wait_ge(sig.ident_zero, 1)
                nc.gpsimd.affine_select(out=ident[:, :], in_=ident[:, :], compare_op=ALU.not_equal,
                                        fill=1.0, base=0, pattern=[[-1, P]],
                                        channel_multiplier=1).then_inc(sig.ident_ready, 1)

            @block.tensor
            def _(pe):
                pe.wait_ge(sig.weights_loaded, 16 * LOADS)
                pe.wait_ge(sig.ident_ready, 1)
                for h in range(H0):
                    pe.transpose(val_bank[h // 4][:, (h % 4) * P:(h % 4 + 1) * P],
                                 fcw[:, h * P:(h + 1) * P], ident[:, :])
                pe.transpose(mid_bank[0][:, 0:P], W3[:, :], ident[:, :]).then_inc(sig.turned, 1)
                pe.wait_ge(sig.turned_read, 1)
                pe.wait_ge(sig.ablk_ready, 1)
                for h in range(H0):
                    pe.matmul(mid_bank[1 + h // 4][:, (h % 4) * P:(h % 4 + 1) * P], fcwT[:, h, :],
                              fpw[:, h, :], start=True, stop=True)
                for h in range(H0):
                    pe.matmul(attn_bank[1][:, 2 * h:2 * h + 2], fcwT[:, h, :], qkw[:, :],
                              start=True, stop=True)
                for h in range(H0):
                    pe.matmul(val_bank[0][:, 0:P], fcb[:, h:h + 1].broadcast_to([P, P]), fpw[:, h, :],
                              start=h == 0, stop=h == H0 - 1)
                pe.matmul(val_bank[1][KROW:KROW + H0, 0:2], fcb[:, :], qkw[:, :], start=True, stop=True)
                pe.matmul(mid_bank[0][:, 0:2 * H3], w3T[:, :], ablk[:, :, :].rearrange("p t h -> p (t h)"),
                          start=True, stop=True).then_inc(sig.folded, 1)

            @block.scalar
            def _(act):
                act.wait_ge(sig.turned, 1)
                for half in range(2):
                    nc.scalar.copy(fcwT[:, 4 * half:4 * half + 4, :].rearrange("p h j -> p (h j)"),
                                   val_bank[half][:, :])
                nc.scalar.copy(w3T[:, :], mid_bank[0][:, 0:P]).then_inc(sig.turned_read, 1)
                act.wait_ge(sig.folded, 1)
                for half in range(2):
                    nc.scalar.copy(Wp[:, 512 * half:512 * half + 512],
                                   mid_bank[1 + half][:, :]).then_inc(sig.constants_ready, 1)

            @block.vector
            def _(dve):
                nc.vector.memset(minus_half[:, :], -0.5)
                for p in range(2):
                    nc.vector.memset(G[p][:, :, :, P:GV], 1.0)
                nc.vector.memset(V3[:, :, :, D3:D3 + 1], 1.0)
                nc.vector.memset(ones[:, :], 1.0)
                nc.vector.memset(B21[:, :], 0.0)
                nc.vector.memset(Wqk[:, :], 0.0)
                nc.vector.memset(Wqk3[:, :], 0.0)
                nc.vector.memset(ablk[:, :, :], 0.0).then_inc(sig.zeroed, 1)
                dve.wait_ge(sig.zeroed, 1)
                dve.wait_ge(sig.weights_loaded, 16 * LOADS)
                for h in range(H3):
                    last = nc.vector.tensor_copy(ablk[h * D3:(h + 1) * D3, :, h],
                                                 acol[h * D3:(h + 1) * D3, :])
                last.then_inc(sig.ablk_ready, 1)
                nc.vector.tensor_copy(B21[0:1, :], b21row[0:1, 0, :]).then_inc(sig.b21_split, 1)
                dve.wait_ge(sig.b21_split, 1)
                nc.vector.tensor_tensor(b21row[0:1, 1, :], b21row[0:1, 0, :], B21[0:1, :],
                                        ALU.subtract).then_inc(sig.b21_split, 1)
                dve.wait_ge(sig.b21_split, 2)
                nc.vector.tensor_copy(B21[KROW:KROW + 1, :], b21row[0:1, 1, :])
                nc.vector.tensor_copy(low[0:1, :], b21row[0:1, 1, :]).then_inc(sig.b21_split, 1)
                dve.wait_ge(sig.b21_split, 3)
                nc.vector.tensor_tensor(B21[2 * KROW:2 * KROW + 1, :], b21row[0:1, 1, :], low[0:1, :],
                                        ALU.subtract)
                dve.wait_ge(sig.ident_ready, 1)
                nc.vector.scalar_tensor_tensor(out=self1[:, :], in0=ident[:, :], scalar=eps[:, 0:1],
                                               in1=ident[:, :], op0=ALU.mult, op1=ALU.add)
                nc.vector.tensor_scalar(self2[:, :], ident[:, :], eps[:, 1:2], None, ALU.mult)
                dve.wait_ge(sig.folded, 1)
                qk = attn_bank[1][:, 0:2 * H0].rearrange("p (h t) -> p t h", t=2)
                for t in range(2):
                    nc.vector.tensor_copy(Wqk[:, t * KROW:t * KROW + H0], qk[:, t, :])
                    nc.vector.tensor_copy(Wqk3[:, t * KROW:t * KROW + H3], mid_bank[0][:, t * H3:(t + 1) * H3])
                nc.vector.tensor_tensor(bias0[:, :], val_bank[0][:, 0:P], fpb[:, :], ALU.add)
                nc.vector.tensor_tensor(qk_sum[KROW:KROW + H0, :], val_bank[1][KROW:KROW + H0, 0:2],
                                        qkb[KROW:KROW + H0, :], ALU.add).then_inc(sig.qk_summed, 1)
                dve.wait_ge(sig.qk_summed, 1)
                nc.vector.reduce_sum(qk_const[KROW:KROW + H0, :], qk_sum[KROW:KROW + H0, :],
                                     AX.X).then_inc(sig.constants_ready, 1)

        with nc.Block() as block:
            @block.sync
            def _(sp):
                def load(it):
                    g, p = it.graph("A"), it.parity("A")
                    if it.had("A", 2):
                        sp.wait_ge(sig.xT_done, it.done("A", 2))
                    if it.had("A", 2):
                        sp.wait_ge(sig.xbias_ready, it.done("A", 2))
                    sp.dma_start(x_in[p][:, :, :],
                                 x[g].rearrange("(b p) d -> p b d", p=P)).then_inc(sig.x_loaded, 16)
                    if it.had("A", 2):
                        sp.wait_ge(sig.adjT_done, it.done("A", 2))
                    sp.dma_start(adj_in[p][:, :, :],
                                 adj[g].rearrange("(b p) m -> p b m", p=P)).then_inc(sig.adj_loaded, 16)

                def spread(it, stage, rows, dram, wide, ready, stored, loaded, used):
                    p = it.parity(stage)
                    sp.wait_ge(ready, it.done(stage))
                    sp.dma_start(dram[p], rows[p][:, :]).then_inc(stored, 16)
                    sp.wait_ge(stored, it.dma_done(stage))
                    if it.had(stage, 2):
                        sp.wait_ge(used, it.done(stage, 2))
                    sp.dma_start(wide[p][:, :, :], dram[p].partition_broadcast(P)).then_inc(loaded, 16)

                def store(it):
                    g, p = it.graph("S"), it.parity("S")
                    sp.wait_ge(ln["F"].norm, it.done("S"))
                    if it.had("S", 1):
                        sp.wait_ge(sig.out_stored, it.dma_done("S", 1))
                    sp.dma_start(out[g].rearrange("(b p) d -> p b d", p=P),
                                 x4[p][:, :, :]).then_inc(sig.out_stored, 16)

                def body(it):
                    a, e, s = (it.active(s) for s in "AES")
                    if a:
                        load(it)
                        spread(it, "A", row_R, R_dram, R, sig.rowR_ready, sig.R_stored,
                               sig.R_loaded, sig.edge_done[3])
                    if e:
                        spread(it, "E", row3_R, R3_dram, R3, sig.rowR3_ready, sig.R3_stored,
                               sig.R3_loaded, sig.edge3_done[1])
                    if s:
                        store(it)

                run_iterations(sp, B, body, [("A", 0), ("E", 0), ("S", 1)])
                sp.wait_ge(sig.out_stored, 16 * B)
                sp.wait_ge(sig.R_loaded, 16 * B)
                sp.wait_ge(sig.R3_loaded, 16 * B)

            @block.tensor
            def _(pe):
                def mid(it, name):
                    k = INDEX[name]
                    back, j = 0, k
                    while it.number is None or back <= it.number:
                        j -= NMID
                        if j < 0:
                            j, back = j + len(PHASES), back + 1
                        if it.active(PHASES[j][1], back):
                            if it.had(PHASES[j][1], back):
                                pe.wait_ge(freed[PHASES[j][0]], it.done(PHASES[j][1], back))
                            break
                    return mid_bank[k % NMID]

                def turn_x(it, name, src, written, value, done):
                    bank = mid(it, name)
                    pe.wait_ge(written, value)
                    for b in range(NB):
                        mm = pe.transpose(bank[:, b * P:(b + 1) * P], src[:, b, :], ident[:, :])
                    mm.then_inc(done, 1)

                def turn_adj(it):
                    bank, p = mid(it, "A_adjT"), it.parity("A")
                    pe.wait_ge(sig.adj_loaded, it.dma_done("A"))
                    for m in range(NB):
                        for n in range(NB):
                            mm = pe.transpose(bank[:, m * N + n * P:m * N + (n + 1) * P],
                                              adj_in[p][:, n, m * P:(m + 1) * P], ident[:, :])
                    mm.then_inc(sig.adjT_done, 1)

                def values(it, c):
                    m, half, p = c % 2, c // 2, it.parity("B")
                    if c == 0:
                        pe.wait_ge(sig.xT_ready, it.done("B"))
                    if c < 2:
                        if it.had("B", 1):
                            pe.wait_ge(sig.val_ready[c + 2], it.done("B", 1))
                    else:
                        pe.wait_ge(sig.val_ready[c - 2], it.done("B"))
                    pe.matmul(val_bank[c % 2][:, :], xT[p][:, m * P:(m + 1) * P],
                              Wp[:, 512 * half:512 * half + 512], start=True, stop=True).then_inc(sig.val_done[c], 1)

                def rows(it, name, stage, turned, w, ready, done):
                    bank, p = mid(it, name), it.parity(stage)
                    pe.wait_ge(ready, it.done(stage))
                    pe.matmul(bank[0:w.shape[1], 0:N], w[:, :], turned[p][:, :],
                              start=True, stop=True).then_inc(done, 1)

                def turn_E(it, name, stage, src, heads, ready, done):
                    pe.wait_ge(sig.constants_ready, 3)
                    bank = mid(it, name)
                    pe.wait_ge(ready, it.done(stage))
                    for b in range(NB):
                        for t in range(2):
                            k = (b * 2 + t) * heads
                            mm = pe.transpose(bank[:, k:k + heads], src[:, t, b * P:(b + 1) * P],
                                              ident[0:heads, 0:heads])
                    mm.then_inc(done, 1)

                def attend(it, u):
                    (g, n), p = UNITS[u], it.parity("P")
                    if u == 0:
                        for c in range(2):
                            pe.wait_ge(sig.weight_ready[c], it.done("P"))
                            pe.wait_ge(sig.val_ready[c], it.done("P"))
                    if u == 2:
                        for c in range(2, 4):
                            pe.wait_ge(sig.weight_ready[c], it.done("P"))
                            pe.wait_ge(sig.val_ready[c], it.done("P"))
                    if u < NO:
                        if it.had("P", 1):
                            pe.wait_ge(sig.attn_read[len(UNITS) - NO + u], it.done("P", 1))
                    else:
                        pe.wait_ge(sig.attn_read[u - NO], it.done("P"))
                    for h in range(*GROUPS[g]):
                        k = (h - GROUPS[g][0]) * GV
                        for m in range(NB):
                            mm = pe.matmul(attn_bank[u % NO][:, k:k + GV], Wt[p][:, m, h, n * P:(n + 1) * P],
                                           G[p][:, m, h, :], start=m == 0, stop=m == NB - 1)
                    mm.then_inc(sig.attn_done[u], 1)

                def aggregate(it, name, stage, xf, hi, lo, own, norm, split, done):
                    bank, g = mid(it, name), it.slot(stage)
                    pe.wait_ge(norm, it.done(stage))
                    pe.wait_ge(split, it.done(stage))
                    for k, part in enumerate((hi, lo)):
                        for m in range(NB):
                            pe.matmul(bank[:, 0:N], part[:, m, :], adjT[:, g, m, :],
                                      start=k == 0 and m == 0, stop=False)
                    for b in range(NB):
                        mm = pe.matmul(bank[:, b * P:(b + 1) * P], xf[:, b, :], own[:, :],
                                       start=False, stop=b == NB - 1)
                    mm.then_inc(done, 1)

                def hidden1(it):
                    bank = mid(it, "C_h")
                    pe.wait_ge(sig.agg1_ready, it.done("C"))
                    for j in range(HID1 // P):
                        mm = pe.matmul(bank[:, j * N:(j + 1) * N], W11[:, j * P:(j + 1) * P], agg1T[:, :],
                                       start=True, stop=True)
                    mm.then_inc(sig.hid1_done, 1)

                def project1(it):
                    bank = mid(it, "C_y")
                    pe.wait_ge(sig.hid1_ready, it.done("C"))
                    for b in range(NB):
                        for j in range(HID1 // P):
                            mm = pe.matmul(bank[:, b * P:(b + 1) * P], hid1T[:, j, b * P:(b + 1) * P],
                                           W12[:, j, :], start=j == 0, stop=j == HID1 // P - 1)
                    mm.then_inc(sig.y1_done, 1)

                def hidden2(it, b):
                    bank = mid(it, f"D_h{b}")
                    pe.matmul(bank[:, :], ones[:, :], B21[:, :], start=True, stop=False)
                    pe.wait_ge(sig.agg2_ready, it.done("D"))
                    pe.matmul(bank[:, :], agg2T[:, b * P:(b + 1) * P], W21[:, :],
                              start=False, stop=True).then_inc(sig.hid2_done[b], 1)

                def turn_sil(it, b):
                    bank = mid(it, f"D_t{b}")
                    pe.wait_ge(sig.sil_done[b], it.done("D"))
                    for j in range(HID2 // P):
                        mm = pe.transpose(bank[:, j * P:(j + 1) * P], tanh2[:, b, j * P:(j + 1) * P], ident[:, :])
                    mm.then_inc(sig.silT_done[b], 1)

                def project2(it):
                    bank = mid(it, "D_y")
                    for b in range(NB):
                        pe.wait_ge(sig.silT_ready[b], it.done("D"))
                        for j in range(HID2 // P):
                            mm = pe.matmul(bank[:, b * P:(b + 1) * P], silT[:, b, j, :], W22[:, j, :],
                                           start=j == 0, stop=j == HID2 // P - 1)
                    mm.then_inc(sig.y2_done, 1)

                def values3(it):
                    bank, p = mid(it, "F_V"), it.parity("F")
                    pe.wait_ge(sig.x3T_ready, it.done("F"))
                    for m in range(NB):
                        mm = pe.matmul(bank[:, m * P:(m + 1) * P], x3T[p][:, m * P:(m + 1) * P], W3[:, :],
                                       start=True, stop=True)
                    mm.then_inc(sig.V3_done, 1)

                def attend3(it, j):
                    bank = mid(it, f"F_O{j}")
                    if j == 0:
                        pe.wait_ge(sig.V3_ready, it.done("F"))
                        for m in range(NB):
                            pe.wait_ge(sig.weight3_ready[m], it.done("F"))
                    for k in range(2):
                        for m in range(NB):
                            mm = pe.matmul(bank[0:D3 + 1, k * N:(k + 1) * N], V3[:, m, 2 * j + k, :],
                                           Wt3[:, m, 2 * j + k, :], start=m == 0, stop=m == NB - 1)
                    mm.then_inc(sig.out3T_done[j], 1)

                def turn_out3(it):
                    pe.wait_ge(sig.constants_ready, 3)
                    bank = mid(it, "F_T")
                    for j in range(2):
                        pe.wait_ge(sig.out3T_ready[j], it.done("F"))
                    for n in range(NB):
                        for h in range(H3):
                            k = (n * H3 + h) * (D3 + 1)
                            c = (h % 2) * N + n * P
                            mm = pe.transpose(bank[:, k:k + D3 + 1], out3T[:, h // 2, c:c + P],
                                              ident[0:D3 + 1, 0:D3 + 1])
                    mm.then_inc(sig.out3_done, 1)

                def body(it):
                    a, b, p, c, d, e, f = (it.active(s) for s in "ABPCDEF")
                    if a:
                        turn_x(it, "A_xT", x_in[it.parity("A")],
                               sig.x_loaded, it.dma_done("A"), sig.xT_done)
                        turn_adj(it)
                    if p:
                        attend(it, 0)
                    if a:
                        rows(it, "A_rows", "A", xT, Wqk, sig.xT_ready, sig.rows_done)
                    if p:
                        attend(it, 1)
                    if e:
                        turn_x(it, "E_xT", x3[it.parity("E")],
                               ln["D"].norm, it.done("E"), sig.x3T_done)
                    if f:
                        values3(it)
                    if d:
                        aggregate(it, "D_agg", "D", x2, x2_hi, x2_lo, self2, ln["C"].norm, sig.x2_split,
                                  sig.agg2_done)
                    if b:
                        values(it, 0)
                    if d:
                        hidden2(it, 0)
                        hidden2(it, 1)
                    if e:
                        rows(it, "E_rows", "E", x3T, Wqk3, sig.x3T_ready, sig.rows3_done)
                    if f:
                        attend3(it, 0)
                    if b:
                        values(it, 1)
                    if p:
                        attend(it, 2)
                    if f:
                        attend3(it, 1)
                    if b:
                        values(it, 2)
                    if p:
                        attend(it, 3)
                    if c:
                        aggregate(it, "C_agg", "C", x1, x1_hi, x1_lo, self1, ln["T"].norm, sig.x1_split,
                                  sig.agg1_done)
                    if d:
                        turn_sil(it, 1)
                        turn_sil(it, 0)
                    if f:
                        turn_out3(it)
                    if c:
                        hidden1(it)
                    if a:
                        turn_E(it, "A_E", "A", row_exp, H0, sig.rowE_ready, sig.E_done)
                    if d:
                        project2(it)
                    if c:
                        project1(it)
                    if e:
                        turn_E(it, "E_E", "E", row3_exp, H3, sig.rowE3_ready, sig.E3_done)
                    if b:
                        values(it, 3)
                    if p:
                        attend(it, 4)
                        attend(it, 5)

                run_iterations(pe, B, body, [("A", 0)])

            @block.scalar
            def _(act):
                def copy_out(it, stage, done, dst, src, ready):
                    act.wait_ge(done, it.done(stage))
                    nc.scalar.copy(dst, src).then_inc(ready, 1)

                def bank(name):
                    return mid_bank[INDEX[name] % NMID]

                def values(it, c):
                    m, half, p = c % 2, c // 2, it.parity("B")
                    act.wait_ge(sig.val_done[c], it.done("B"))
                    nc.scalar.copy(G[p][:, m, 4 * half:4 * half + 4, 0:P],
                                   val_bank[c % 2][:, :].rearrange("p (h e) -> p h e", e=P)
                                   ).then_inc(sig.val_ready[c], 1)

                def exponentials(it, stage, slope, row, row_R, row_E, read, stored, ready, E_ready):
                    p = it.parity(stage)
                    act.wait_ge(read, it.done(stage))
                    if it.had(stage, 2):
                        act.wait_ge(stored, it.dma_done(stage, 2))
                    nc.scalar.activation(row_R[p][:, :], row[:, 0, :], ACT.Exp, scale=1.0 - slope).then_inc(ready, 1)
                    nc.scalar.activation(row_E[:, 0, :], row[:, 1, :], ACT.Exp)
                    nc.scalar.activation(row_E[:, 1, :], row[:, 1, :], ACT.Exp, scale=slope).then_inc(E_ready, 1)

                def relu1(it):
                    act.wait_ge(sig.hid1_done, it.done("C"))
                    for j in range(HID1 // P):
                        last = nc.scalar.activation(hid1T[:, j, :], bank("C_h")[:, j * N:(j + 1) * N],
                                                    ACT.Relu, bias=B11[:, j:j + 1])
                    last.then_inc(sig.hid1_ready, 1)

                def squares(it, b):
                    act.wait_ge(sig.hid2_done[b], it.done("D"))
                    if it.had("D", 1):
                        act.wait_ge(sig.gate_done[b], it.done("D", 1))
                    nc.scalar.copy(hid2[:, b, :], bank(f"D_h{b}")[:, :]).then_inc(sig.hid2_ready[b], 1)
                    nc.scalar.activation(tanh2[:, b, :], bank(f"D_h{b}")[:, :], ACT.Square,
                                         accum_out=sumsq[:, b:b + 1]).then_inc(sig.sumsq_done[b], 1)

                def edges(it, c):
                    m, half, p = c % 2, c // 2, it.parity("B")
                    if not ACT0[c]:
                        return
                    act.wait_ge(sig.R_loaded, it.dma_done("B"))
                    act.wait_ge(sig.E_ready, it.done("B"))
                    if it.had("B", 2):
                        act.wait_ge(sig.attn_done[5], it.done("B", 2))
                    for h in range(4 * half, 4 * half + 4):
                        last = nc.scalar.activation(Wt[p][:, m, h, :], R[p][:, h, :], ACT.Relu,
                                                    scale=E[p][:, m, 0, h:h + 1], bias=nE[p][:, m, h:h + 1])
                    last.then_inc(sig.edge_done[c], 1)

                def edges3(it, m):
                    p = it.parity("F")
                    if not ACT3[m]:
                        return
                    act.wait_ge(sig.R3_loaded, it.dma_done("F"))
                    act.wait_ge(sig.E3_ready, it.done("F"))
                    if it.had("F", 1):
                        act.wait_ge(sig.out3T_done[1], it.done("F", 1))
                    for h in range(H3):
                        last = nc.scalar.activation(Wt3[:, m, h, :], R3[p][:, h, :], ACT.Relu,
                                                    scale=E3[p][:, m, 0, h:h + 1], bias=nE3[p][:, m, h:h + 1])
                    last.then_inc(sig.edge3_done[m], 1)

                def columns(it, stage, name, E, nE, heads, turned, ready):
                    p = it.parity(stage)
                    act.wait_ge(turned, it.done(stage))
                    src = bank(name)[:, 0:NB * 2 * heads].rearrange("p (b t h) -> p b t h", b=NB, t=2)
                    nc.scalar.copy(E[p][:, :, :, :], src)
                    nc.scalar.mul(nE[p][:, :, :], src[:, :, 1, :], -1.0).then_inc(ready, 1)

                def tanhs(it, b):
                    act.wait_ge(sig.half_done, it.done("D"))
                    act.wait_ge(sig.gate_done[b], it.done("D"))
                    nc.scalar.activation(tanh2[:, b, :], gate[:, b, :], ACT.Tanh,
                                         scale=half_rms[:, b:b + 1]).then_inc(sig.tanh_done[b], 1)

                def tanh0(it):
                    act.wait_ge(sig.zsum_ready, it.done("C"))
                    nc.scalar.activation(sg0[:, :, :], zsum[:, :, :], ACT.Tanh, scale=0.5).then_inc(sig.sg0_ready, 1)

                def body(it):
                    a, b, c, d, e, f = (it.active(s) for s in "ABCDEF")
                    if f:
                        edges3(it, 1)
                    if a:
                        copy_out(it, "A", sig.xT_done, xT[it.parity("A")][:, :], bank("A_xT")[:, 0:N], sig.xT_ready)
                        copy_out(it, "A", sig.adjT_done,
                                 adjT[:, it.slot("A"), :, :],
                                 bank("A_adjT")[:, :].rearrange("p (m n) -> p m n", m=NB), sig.adjT_ready)
                    if b:
                        edges(it, 1)
                    if f:
                        edges3(it, 0)
                    if d:
                        copy_out(it, "D", sig.agg2_done, agg2T[:, :], bank("D_agg")[:, 0:N], sig.agg2_ready)
                    if e:
                        copy_out(it, "E", sig.x3T_done, x3T[it.parity("E")][:, :], bank("E_xT")[:, 0:N],
                                 sig.x3T_ready)
                    if f:
                        copy_out(it, "F", sig.V3_done, V3[:, :, :, 0:D3],
                                 bank("F_V")[:, 0:N].rearrange("p (m h e) -> p m h e", m=NB, h=H3), sig.V3_ready)
                    if a:
                        exponentials(it, "A", A0, row_in, row_R, row_exp, sig.rows_read, sig.R_stored,
                                     sig.rowR_ready, sig.rowE_ready)
                    if b:
                        values(it, 0)
                    if d:
                        squares(it, 0)
                    if c:
                        tanh0(it)
                    if d:
                        squares(it, 1)
                    if b:
                        edges(it, 2)
                        values(it, 1)
                    if e:
                        exponentials(it, "E", A3, row3_in, row3_R, row3_exp, sig.rows3_read, sig.R3_stored,
                                     sig.rowR3_ready, sig.rowE3_ready)
                    if d:
                        tanhs(it, 1)
                        tanhs(it, 0)
                    if f:
                        copy_out(it, "F", sig.out3T_done[0], out3T[:, 0, :], bank("F_O0")[0:D3 + 1, :],
                                 sig.out3T_ready[0])
                    if b:
                        edges(it, 0)
                    if f:
                        copy_out(it, "F", sig.out3T_done[1], out3T[:, 1, :], bank("F_O1")[0:D3 + 1, :],
                                 sig.out3T_ready[1])
                    if c:
                        copy_out(it, "C", sig.agg1_done, agg1T[:, :], bank("C_agg")[:, 0:N], sig.agg1_ready)
                    if d:
                        copy_out(it, "D", sig.silT_done[1], silT[:, 1, :, :].rearrange("p j n -> p (j n)"),
                                 bank("D_t1")[:, :], sig.silT_ready[1])
                        copy_out(it, "D", sig.silT_done[0], silT[:, 0, :, :].rearrange("p j n -> p (j n)"),
                                 bank("D_t0")[:, :], sig.silT_ready[0])
                    if c:
                        relu1(it)
                    if a:
                        columns(it, "A", "A_E", E, nE, H0, sig.E_done, sig.E_ready)
                    if b:
                        edges(it, 3)
                        values(it, 2)
                    if e:
                        columns(it, "E", "E_E", E3, nE3, H3, sig.E3_done, sig.E3_ready)
                    if b:
                        values(it, 3)

                run_iterations(act, B, body, [("A", 2), ("E", 2), ("B", 0), ("F", 0)])

            @block.vector
            def _(dve):
                def bank(name):
                    return mid_bank[INDEX[name] % NMID]

                def limits(it):
                    g = it.slot("A")
                    dve.wait_ge(sig.adjT_ready, it.done("A"))
                    nc.vector.tensor_scalar(limit[:, g, :, :], adjT[:, g, :, :], BIG, FLOOR,
                                            ALU.mult, ALU.add).then_inc(sig.limit_ready, 1)

                def row_terms(it, name, stage, slope, row, kmax, kq, const, heads, done, max_done, kq_done, read):
                    rows = bank(name)
                    keys = slice(KROW, KROW + heads)
                    dve.wait_ge(done, it.done(stage))
                    nc.vector.reduce_max(kmax[keys, 0:1], rows[keys, 0:N], AX.X).then_inc(max_done, 1)
                    dve.wait_ge(max_done, it.done(stage))
                    nc.vector.tensor_scalar(kq[:, 0:1], kmax[keys, 0:1], const, None, ALU.add).then_inc(kq_done, 1)
                    nc.vector.tensor_scalar(row[:, 1, :], rows[keys, 0:N], kmax[keys, 0:1], None, ALU.subtract)
                    dve.wait_ge(kq_done, it.done(stage))
                    nc.vector.tensor_scalar(row[:, 0, :], rows[0:heads, 0:N], kq[:, 0:1], CLAMP / (1 - slope),
                                            ALU.add, ALU.min).then_inc(read, 1)

                def weights(it, c):
                    m, half, p, g = c % 2, c // 2, it.parity("B"), it.slot("B")
                    if c == 0:
                        dve.wait_ge(sig.limit_ready, it.done("B"))
                        dve.wait_ge(sig.E_ready, it.done("B"))
                    if ACT0[c]:
                        dve.wait_ge(sig.edge_done[c], it.done("B"))
                        for h in range(4 * half, 4 * half + 4):
                            w = Wt[p][:, m, h, :]
                            last = nc.vector.scalar_tensor_tensor(out=w, in0=w, scalar=E[p][:, m, 1, h:h + 1],
                                                                  in1=limit[:, g, m, :], op0=ALU.add, op1=ALU.min)
                        last.then_inc(sig.weight_ready[c], 1)
                    else:
                        dve.wait_ge(sig.R_loaded, it.dma_done("B"))
                        if it.had("B", 2):
                            dve.wait_ge(sig.attn_done[5], it.done("B", 2))
                        for h in range(4 * half, 4 * half + 4):
                            last = nc.vector.tensor_scalar(Wt[p][:, m, h, :], R[p][:, h, :], E[p][:, m, 0, h:h + 1],
                                                           E[p][:, m, 1, h:h + 1], ALU.mult, ALU.max)
                        last.then_inc(sig.edge_done[c], 1)
                        dve.wait_ge(sig.edge_done[c], it.done("B"))
                        w = Wt[p][:, m, 4 * half:4 * half + 4, :]
                        nc.vector.tensor_tensor(w, w, limit[:, g, m, :].unsqueeze(1).broadcast_to([P, 4, N]),
                                                ALU.min).then_inc(sig.weight_ready[c], 1)

                def weights3(it, m):
                    p, g = it.parity("F"), it.slot("F")
                    dve.wait_ge(sig.E3_ready, it.done("F"))
                    if ACT3[m]:
                        dve.wait_ge(sig.edge3_done[m], it.done("F"))
                        for h in range(H3):
                            last = nc.vector.scalar_tensor_tensor(
                                out=Wt3[:, m, h, :], in0=Wt3[:, m, h, :], scalar=E3[p][:, m, 1, h:h + 1],
                                in1=limit[:, g, m, :], op0=ALU.add, op1=ALU.min)
                        last.then_inc(sig.weight3_ready[m], 1)
                    else:
                        dve.wait_ge(sig.R3_loaded, it.dma_done("F"))
                        if it.had("F", 1):
                            dve.wait_ge(sig.out3T_done[1], it.done("F", 1))
                        for h in range(H3):
                            last = nc.vector.tensor_scalar(Wt3[:, m, h, :], R3[p][:, h, :], E3[p][:, m, 0, h:h + 1],
                                                           E3[p][:, m, 1, h:h + 1], ALU.mult, ALU.max)
                        last.then_inc(sig.edge3_done[m], 1)
                        dve.wait_ge(sig.edge3_done[m], it.done("F"))
                        nc.vector.tensor_tensor(Wt3[:, m, :, :], Wt3[:, m, :, :],
                                                limit[:, g, m, :].unsqueeze(1).broadcast_to([P, H3, N]),
                                                ALU.min).then_inc(sig.weight3_ready[m], 1)

                def normalise(it, u):
                    (g, n), p = UNITS[u], it.parity("P")
                    lo, hi = GROUPS[g]
                    if u == 0:
                        if it.had("P", 2):
                            dve.wait_ge(sig.zsum_ready, it.done("P", 2))
                    dve.wait_ge(sig.attn_done[u], it.done("P"))
                    o = attn_bank[u % NO][:, 0:(hi - lo) * GV].rearrange("p (h e) -> p h e", e=GV)
                    nc.vector.reciprocal(rden[:, n, lo:hi], o[:, :, P]).then_inc(sig.attn_sum[u], 1)
                    dve.wait_ge(sig.attn_sum[u], it.done("P"))
                    nc.vector.tensor_tensor(T[p][:, n, lo:hi, :], o[:, :, 0:P],
                                            rden[:, n, lo:hi].unsqueeze(2).broadcast_to([P, hi - lo, P]),
                                            ALU.mult).then_inc(sig.attn_read[u], 1)

                def statistics(it, s, stage):
                    dve.wait_ge(ln[s].y, it.done(stage))
                    for b in range(NB):
                        last = nc.vector.bn_stats(stats[s][:, b, :], y[s][:, b, :])
                    last.then_inc(ln[s].stats, 1)

                def moments(it, s, stage):
                    dve.wait_ge(sig.constants_ready, 3)
                    dve.wait_ge(ln[s].stats, it.done(stage))
                    for b in range(NB):
                        last = nc.vector.bn_aggr(mv[s][:, b, :], stats[s][:, b, :])
                    last.then_inc(ln[s].mv, 1)

                def norm(it, s, stage, dst):
                    dve.wait_ge(ln[s].rstd, it.done(stage))
                    for b in range(NB):
                        last = nc.vector.tensor_scalar(dst[:, b, :], y[s][:, b, :], mv[s][:, b, 0:1],
                                                       rstd[s][:, b:b + 1], ALU.subtract, ALU.mult)
                    last.then_inc(ln[s].norm, 1)

                def residual0(it):
                    p = it.parity("C")
                    dve.wait_ge(sig.sg0_ready, it.done("C"))
                    nc.vector.scalar_tensor_tensor(out=y["T"][:, :, :], in0=sg0[:, :, :], scalar=0.5,
                                                   in1=x_half[p][:, :, :], op0=ALU.mult,
                                                   op1=ALU.add).then_inc(ln["T"].y, 1)

                def residual1(it):
                    dve.wait_ge(sig.y1_done, it.done("C"))
                    dve.wait_ge(sig.x1b_ready, it.done("C"))
                    nc.vector.tensor_tensor(y["C"][:, :, :],
                                            bank("C_y")[:, 0:N].rearrange("p (b e) -> p b e", b=NB),
                                            x1b[:, :, :], ALU.add).then_inc(ln["C"].y, 1)

                def silu2(it, b):
                    dve.wait_ge(sig.tanh_done[b], it.done("D"))
                    nc.vector.scalar_tensor_tensor(out=tanh2[:, b, :], in0=tanh2[:, b, :], scalar=1.0,
                                                   in1=gate[:, b, :], op0=ALU.add,
                                                   op1=ALU.mult).then_inc(sig.sil_done[b], 1)

                def residual2(it):
                    dve.wait_ge(sig.y2_done, it.done("D"))
                    dve.wait_ge(sig.x2b_ready, it.done("D"))
                    for b in range(NB):
                        last = nc.vector.scalar_tensor_tensor(
                            out=y["D"][:, b, :], in0=bank("D_y")[:, b * P:(b + 1) * P],
                            scalar=half_rms[:, b:b + 1], in1=x2b[:, b, :], op0=ALU.mult, op1=ALU.add)
                    last.then_inc(ln["D"].y, 1)

                def residual3(it):
                    p = it.parity("F")
                    dve.wait_ge(sig.out3_done, it.done("F"))
                    o = bank("F_T")[:, 0:NB * H3 * (D3 + 1)].rearrange("p (k e) -> p k e", e=D3 + 1)
                    nc.vector.reciprocal(rden3[:, :, :].rearrange("p b h -> p (b h)"),
                                         o[:, :, D3]).then_inc(sig.sum3_done, 1)
                    dve.wait_ge(sig.sum3_done, it.done("F"))
                    nc.vector.tensor_tensor(
                        out3[:, :, :].rearrange("p b (h e) -> p (b h) e", h=H3), o[:, :, 0:D3],
                        rden3[:, :, :].rearrange("p b h -> p (b h)").unsqueeze(2).broadcast_to([P, NB * H3, D3]),
                        ALU.mult).then_inc(sig.out3_read, 1)
                    dve.wait_ge(sig.out3_read, it.done("F"))
                    nc.vector.tensor_tensor(y["F"][:, :, :], out3[:, :, :], x3[p][:, :, :],
                                            ALU.add).then_inc(ln["F"].y, 1)

                def body(it):
                    a, b, p, c, d, e, f = (it.active(s) for s in "ABPCDEF")
                    if a:
                        row_terms(it, "A_rows", "A", A0, row_in, kmax, kq, qk_const[KROW:KROW + H0, 0:1], H0,
                                  sig.rows_done, sig.kmax_done, sig.kq_done, sig.rows_read)
                    if f:
                        weights3(it, 1)
                        weights3(it, 0)
                    if p:
                        normalise(it, 0)
                        normalise(it, 1)
                    if c:
                        residual0(it)
                    if a:
                        limits(it)
                    if c:
                        statistics(it, "T", "C")
                        moments(it, "T", "C")
                    if e:
                        row_terms(it, "E_rows", "E", A3, row3_in, kmax3, kq3, 0.0, H3, sig.rows3_done,
                                  sig.kmax3_done, sig.kq3_done, sig.rows3_read)
                    if c:
                        if it.had("C", 1):
                            dve.wait_ge(sig.agg1_done, it.done("C", 1))
                            dve.wait_ge(sig.x1b_ready, it.done("C", 1))
                        norm(it, "T", "C", x1)
                    if b:
                        weights(it, 1)
                    if p:
                        normalise(it, 2)
                    if d:
                        silu2(it, 1)
                        silu2(it, 0)
                    if b:
                        weights(it, 2)
                    if p:
                        normalise(it, 3)
                    if f:
                        residual3(it)
                    if b:
                        weights(it, 0)
                    if f:
                        statistics(it, "F", "F")
                    if d:
                        residual2(it)
                    if f:
                        moments(it, "F", "F")
                    if c:
                        residual1(it)
                        statistics(it, "C", "C")
                        moments(it, "C", "C")
                    if d:
                        statistics(it, "D", "D")
                        moments(it, "D", "D")
                    if p:
                        normalise(it, 4)
                    if c:
                        if it.had("C", 1):
                            dve.wait_ge(sig.agg2_done, it.done("C", 1))
                            dve.wait_ge(sig.x2b_ready, it.done("C", 1))
                        norm(it, "C", "C", x2)
                    if p:
                        normalise(it, 5)
                    if f:
                        if it.had("F", 2):
                            dve.wait_ge(sig.out_stored, it.dma_done("F", 2))
                        norm(it, "F", "F", x4[it.parity("F")])
                    if d:
                        norm(it, "D", "D", x3[it.parity("D")])
                    if b:
                        weights(it, 3)

                run_iterations(dve, B, body, [("B", 0), ("F", 0), ("F", 2)])

            @block.gpsimd
            def _(pool):
                def head_sum(it):
                    t = T[it.parity("C")]
                    pool.wait_ge(sig.attn_read[5], it.done("C"))
                    nc.gpsimd.tensor_tensor(t[:, :, 0:4, :], t[:, :, 0:4, :], t[:, :, 4:8, :],
                                            ALU.add).then_inc(sig.tree1_done, 1)
                    pool.wait_ge(sig.tree1_done, it.done("C"))
                    nc.gpsimd.tensor_tensor(t[:, :, 0:2, :], t[:, :, 0:2, :], t[:, :, 2:4, :],
                                            ALU.add).then_inc(sig.tree2_done, 1)
                    pool.wait_ge(sig.tree2_done, it.done("C"))
                    nc.gpsimd.tensor_tensor(t[:, :, 0, :], t[:, :, 0, :], t[:, :, 1, :],
                                            ALU.add).then_inc(sig.tree3_done, 1)
                    pool.wait_ge(sig.tree3_done, it.done("C"))
                    nc.gpsimd.tensor_tensor(zsum[:, :, :], t[:, :, 0, :], x_bias[it.parity("C")][:, :, :],
                                            ALU.add).then_inc(sig.zsum_ready, 1)

                def x_terms(it):
                    p = it.parity("B")
                    pool.wait_ge(sig.constants_ready, 3)
                    if it.had("B", 2):
                        pool.wait_ge(ln["T"].y, it.done("B", 2))
                    pool.wait_ge(sig.x_loaded, it.dma_done("B"))
                    nc.gpsimd.tensor_scalar(x_half[p][:, :, :], x_in[p][:, :, :], 0.5, 1.0, ALU.add, ALU.mult)
                    nc.gpsimd.tensor_tensor(x_bias[p][:, :, :], x_in[p][:, :, :],
                                            bias0[:, :].unsqueeze(1).broadcast_to([P, NB, P]),
                                            ALU.add).then_inc(sig.xbias_ready, 1)

                def rsqrt_var(it, s, stage):
                    pool.wait_ge(sig.constants_ready, 3)
                    pool.wait_ge(ln[s].mv, it.done(stage))
                    nc.gpsimd.tensor_scalar(ve[s][:, :], mv[s][:, :, 1], LN_EPS, 1.0, ALU.add,
                                            ALU.mult).then_inc(ln[s].ve, 1)
                    pool.wait_ge(ln[s].ve, it.done(stage))
                    nc.gpsimd.tensor_tensor(rstd[s][:, :], ve[s][:, :], minus_half[:, :],
                                            ALU.pow).then_inc(ln[s].rstd, 1)

                def split(it, stage, src, hi, lo, agg_done, norm_done, hi_done, done):
                    pool.wait_ge(sig.constants_ready, 3)
                    pool.wait_ge(norm_done, it.done(stage))
                    if it.had(stage, 1):
                        pool.wait_ge(agg_done, it.done(stage, 1))
                    nc.gpsimd.tensor_copy(hi[:, :, :], src[:, :, :]).then_inc(hi_done, 1)
                    pool.wait_ge(hi_done, it.done(stage))
                    nc.gpsimd.tensor_tensor(lo[:, :, :], src[:, :, :], hi[:, :, :], ALU.subtract).then_inc(done, 1)

                def add_bias(it, stage, dst, src, bias, written, y_done, done):
                    pool.wait_ge(written, it.done(stage))
                    if it.had(stage, 1):
                        pool.wait_ge(y_done, it.done(stage, 1))
                    nc.gpsimd.tensor_tensor(dst[:, :, :], src[:, :, :],
                                            bias[:, :].unsqueeze(1).broadcast_to([P, NB, P]),
                                            ALU.add).then_inc(done, 1)

                def gates(it, b):
                    pool.wait_ge(sig.hid2_ready[b], it.done("D"))
                    if it.had("D", 1):
                        pool.wait_ge(sig.sil_done[b], it.done("D", 1))
                    nc.gpsimd.tensor_tensor(gate[:, b, :], hid2[:, b, :], RMSW[:, :],
                                            ALU.mult).then_inc(sig.gate_done[b], 1)

                def rsqrt_rms(it):
                    pool.wait_ge(sig.constants_ready, 3)
                    if it.had("D", 1):
                        pool.wait_ge(ln["D"].y, it.done("D", 1))
                    for b in range(NB):
                        pool.wait_ge(sig.sumsq_done[b], it.done("D"))
                    nc.gpsimd.tensor_scalar(msq[:, :], sumsq[:, :], 1.0 / HID2, RMS_EPS, ALU.mult,
                                            ALU.add).then_inc(sig.msq_done, 1)
                    pool.wait_ge(sig.msq_done, it.done("D"))
                    nc.gpsimd.tensor_tensor(rms[:, :], msq[:, :], minus_half[:, :],
                                            ALU.pow).then_inc(sig.rms_done, 1)
                    pool.wait_ge(sig.constants_ready, 3)
                    pool.wait_ge(sig.rms_done, it.done("D"))
                    nc.gpsimd.tensor_scalar(half_rms[:, :], rms[:, :], 0.5, 1.0, ALU.mult,
                                            ALU.mult).then_inc(sig.half_done, 1)

                def body(it):
                    b, c, d, f = (it.active(s) for s in "BCDF")
                    if c:
                        head_sum(it)
                    if d:
                        gates(it, 0)
                        gates(it, 1)
                    if c:
                        rsqrt_var(it, "T", "C")
                    if d:
                        rsqrt_rms(it)
                    if c:
                        split(it, "C", x1, x1_hi, x1_lo, sig.agg1_done, ln["T"].norm, sig.x1_hi_done, sig.x1_split)
                        add_bias(it, "C", x1b, x1, B12, ln["T"].norm, ln["C"].y, sig.x1b_ready)
                    if d:
                        add_bias(it, "D", x2b, x2, B22, ln["C"].norm, ln["D"].y, sig.x2b_ready)
                    if b:
                        x_terms(it)
                    if f:
                        rsqrt_var(it, "F", "F")
                    if c:
                        rsqrt_var(it, "C", "C")
                    if d:
                        rsqrt_var(it, "D", "D")
                    if c:
                        split(it, "C", x2, x2_hi, x2_lo, sig.agg2_done, ln["C"].norm, sig.x2_hi_done, sig.x2_split)

                run_iterations(pool, B, body, [("B", 0)])


_INS = ["x", "adj", "L0_gnn_fc_w", "L0_gnn_fc_b", "L0_gnn_q_w", "L0_gnn_q_b", "L0_gnn_k_w", "L0_gnn_k_b",
        "L0_gnn_fp_w", "L0_gnn_fp_b", "L1_gnn_eps", "L1_gnn_W1", "L1_gnn_b1", "L1_gnn_W2", "L1_gnn_b2",
        "L2_gnn_epsilon", "L2_gnn_W1", "L2_gnn_b1", "L2_gnn_rms_weight", "L2_gnn_W2", "L2_gnn_b2",
        "L3_gnn_W", "L3_gnn_a"]


def kernel(**inputs):
    import numpy as _np
    import concourse.bacc as _bacc
    from concourse import mybir as _mybir
    from concourse.bass_utils import run_bass_kernel_spmd as _run

    nc = _bacc.Bacc("TRN2", target_bir_lowering=False, num_devices=1)
    arrays, args = {}, []
    laid_out = {
        "L0_gnn_fc_b": lambda v: v.reshape(H0, P).T,
        "L1_gnn_b1": lambda v: v.reshape(HID1 // P, P).T,
        "L3_gnn_a": lambda v: v.reshape(H3, 2, D3).transpose(0, 2, 1).reshape(P, 2),
    }
    for name in _INS:
        a = _np.asarray(inputs[name])
        a = _np.ascontiguousarray(laid_out[name](a) if name in laid_out else a)
        a = a.reshape(a.shape or (1,))
        arrays[f"in_{name}_dram"] = a
        args.append(nc.dram_tensor(f"in_{name}_dram", a.shape, _mybir.dt.from_np(a.dtype), kind="ExternalInput").ap())
    out = nc.dram_tensor("out_dram", inputs["x"].shape, _mybir.dt.float32, kind="ExternalOutput").ap()
    gnn_stack(nc, *args, out)
    r = _run(nc, [arrays], core_ids=[0])
    return r.results[0]["out_dram"]
```

```python
from contextlib import ExitStack

import concourse.bass as bass
from concourse import mybir

ALU = mybir.AluOpType
ACT = mybir.ActivationFunctionType
AX = mybir.AxisListType
F32 = mybir.dt.float32
F16 = mybir.dt.float16
BF16 = mybir.dt.bfloat16

P = 128
H0, H3 = 8, 4
A0, A3 = 0.01, 0.2
D3 = P // H3
HID1, HID2 = 256, 512
LN_EPS, RMS_EPS = 1e-5, 1e-6
EPS = dict(T=4 * LN_EPS, C=LN_EPS, D=LN_EPS, F=LN_EPS)
CLAMP = 70.0
BIG = 2.0 ** 127
FLOOR = 2.0 ** -80
HALF = P // 2
GV = P + 1
GROUPS = ((0, 3), (3, 6), (6, 8))
UNITS = [(g, nb) for g in range(3) for nb in range(2)]
NO = 2

SKEW = dict(L=0, A=1, B=2, P=3, C=4, D=5, E=6, F=7, S=8)
DEPTH = max(SKEW.values())
RING = 8

PHASES = [
    ("A_xT", "A"), ("A_adjT", "A"), ("D_agg", "D"), ("D_h0", "D"), ("D_h1", "D"),
    ("E_xT", "E"), ("F_V", "F"), ("A_rows", "A"), ("E_rows", "E"), ("F_O", "F"),
    ("A_E", "A"), ("C_agg", "C"), ("D_t0", "D"), ("F_T", "F"), ("C_h", "C"),
    ("D_t1", "D"), ("C_y", "C"), ("E_E", "E"), ("D_y", "D"),
]
NMID = 4
KROW = 32
INDEX = {name: k for k, (name, _) in enumerate(PHASES)}


class Signals:

    def __init__(self, new):
        def each(name, n):
            return [new(f"{name}{k}") for k in range(n)]

        self.fold_loaded, self.fpw_loaded, self.weights_loaded = new("fold_loaded"), new("fpw_loaded"), new("weights_loaded")
        self.ident_zero, self.ident_ready = new("ident_zero"), new("ident_ready")
        self.turned, self.turned_read = new("turned"), new("turned_read")
        self.qk_folded, self.qk_ready, self.folded = new("qk_folded"), new("qk_ready"), new("folded")
        self.zeroed, self.ablk_ready = new("zeroed"), new("ablk_ready")
        self.qk_summed, self.constants_ready = new("qk_summed"), new("constants_ready")
        self.x_loaded, self.adj_loaded = new("x_loaded"), new("adj_loaded")
        self.xT_done, self.xT_ready = new("xT_done"), new("xT_ready")
        self.adjT_done, self.adjT_ready, self.limit_ready = new("adjT_done"), new("adjT_ready"), new("limit_ready")
        self.rows_done, self.rows_read = new("rows_done"), new("rows_read")
        self.kmax_done, self.kq_done = new("kmax_done"), new("kq_done")
        self.rowR_ready, self.rowE_ready = new("rowR_ready"), new("rowE_ready")
        self.R_stored, self.R_loaded = new("R_stored"), new("R_loaded")
        self.E_done, self.E_ready = new("E_done"), new("E_ready")
        self.val_done, self.val_ready = each("val_done", 4), each("val_ready", 4)
        self.edge_done, self.weight_ready = each("edge_done", 4), each("weight_ready", 4)
        self.xbias_ready = new("xbias_ready")
        self.attn_done, self.attn_sum, self.attn_read = each("attn_done", 6), each("attn_sum", 6), each("attn_read", 6)
        self.tree1_done, self.tree2_done, self.tree3_done = new("tree1_done"), new("tree2_done"), new("tree3_done")
        self.zsum_ready, self.sg0_ready = new("zsum_ready"), new("sg0_ready")
        self.x1_hi_done, self.x1_split, self.x1b_ready = new("x1_hi_done"), new("x1_split"), new("x1b_ready")
        self.agg1_done, self.agg1_ready = new("agg1_done"), new("agg1_ready")
        self.hid1_done, self.hid1_ready, self.y1_done = new("hid1_done"), new("hid1_ready"), new("y1_done")
        self.x2_hi_done, self.x2_split, self.x2b_ready = new("x2_hi_done"), new("x2_split"), new("x2b_ready")
        self.agg2_done, self.agg2_ready = new("agg2_done"), new("agg2_ready")
        self.hid2_done, self.hid2_ready = each("hid2_done", 2), each("hid2_ready", 2)
        self.sumsq_done, self.gate_done = each("sumsq_done", 2), each("gate_done", 2)
        self.msq_done, self.rms_done, self.half_done = new("msq_done"), new("rms_done"), new("half_done")
        self.tanh_done, self.sil_done = each("tanh_done", 2), each("sil_done", 2)
        self.silT_done, self.silT_ready = each("silT_done", 2), each("silT_ready", 2)
        self.y2_done = new("y2_done")
        self.x3T_done, self.x3T_ready = new("x3T_done"), new("x3T_ready")
        self.rows3_done, self.kmax3_done, self.rows3_read = new("rows3_done"), new("kmax3_done"), new("rows3_read")
        self.kq3_done = new("kq3_done")
        self.rowR3_ready, self.rowE3_ready = new("rowR3_ready"), new("rowE3_ready")
        self.R3_stored, self.R3_loaded = new("R3_stored"), new("R3_loaded")
        self.E3_done, self.E3_ready = new("E3_done"), new("E3_ready")
        self.V3_done, self.V3_ready = new("V3_done"), new("V3_ready")
        self.edge3_done, self.weight3_ready = each("edge3_done", 2), each("weight3_ready", 2)
        self.out3T_done, self.out3T_ready = new("out3T_done"), new("out3T_ready")
        self.out3_done, self.sum3_done, self.out3_read = new("out3_done"), new("sum3_done"), new("out3_read")
        self.out_stored = new("out_stored")
        self.ln = {s: NormSignals(new, s) for s in "TCDF"}

    def freed(self):
        return {"A_xT": self.xT_ready, "A_adjT": self.adjT_ready, "A_rows": self.rowE_ready, "A_E": self.E_ready,
                "C_agg": self.agg1_ready, "C_h": self.hid1_ready, "C_y": self.ln["C"].y,
                "D_agg": self.agg2_ready, "D_h0": self.hid2_ready[0], "D_h1": self.hid2_ready[1],
                "D_t0": self.silT_ready[0], "D_t1": self.silT_ready[1], "D_y": self.ln["D"].y,
                "E_xT": self.x3T_ready, "E_rows": self.rowE3_ready, "E_E": self.E3_ready,
                "F_V": self.V3_ready, "F_O": self.out3T_ready,
                "F_T": self.out3_read}


class NormSignals:

    def __init__(self, new, s):
        self.y, self.stats, self.mv = new(f"y_{s}"), new(f"stats_{s}"), new(f"mv_{s}")
        self.ve, self.rstd, self.norm = new(f"ve_{s}"), new(f"rstd_{s}"), new(f"norm_{s}")


class Iteration:

    def __init__(self, eng, graphs, number=None, loop=None):
        self.eng, self.graphs, self.number = eng, graphs, number
        self.base, self.kept = loop, {}

    def second(self):
        it = Iteration(self.eng, self.graphs)
        it.base, it.kept, it.shift = self.base, self.kept, 1
        return it

    shift = 0

    def plus(self, c):
        if self.number is not None:
            return self.number + c
        c += self.shift
        if c not in self.kept:
            self.kept[c] = self.eng.snap(self.base + c)
            self.eng.compute_val(self.kept[c])
        return self.kept[c]

    def plus16(self, c):
        if self.number is not None:
            return 16 * (self.number + c)
        c += self.shift
        if ("16", c) not in self.kept:
            self.kept["16", c] = self.eng.snap(self.base * 16 + 16 * c)
            self.eng.compute_val(self.kept["16", c])
        return self.kept["16", c]

    def active(self, stage, back=0):
        return self.number is None or 0 <= self.number - back - SKEW[stage] < self.graphs

    def parity(self, stage):
        i = self.number if self.number is not None else self.shift
        return (i - SKEW[stage]) % 2

    def graph(self, stage):
        return self.plus(-SKEW[stage])

    def slot(self, stage):
        c = -SKEW[stage]
        if self.number is not None:
            return (self.number + c) % RING
        c += self.shift
        if ("slot", c) not in self.kept:
            self.kept["slot", c] = self.eng.snap((self.base + c) % RING)
            self.eng.compute_val(self.kept["slot", c])
        return self.kept["slot", c]

    def had(self, stage, ago):
        return self.number is None or self.number - SKEW[stage] - ago >= 0

    def done(self, stage, ago=0):
        return self.plus(1 - SKEW[stage] - ago)

    def dma_done(self, stage, ago=0):
        return self.plus16(1 - SKEW[stage] - ago)


def run_iterations(eng, graphs, body, dma_waits=()):
    first = SKEW["F"] + 3
    for i in range(first):
        body(Iteration(eng, graphs, number=i))
    with eng.Fori(first // 2, graphs // 2) as pair:
        it = Iteration(eng, graphs, loop=pair * 2)
        for c in range(-DEPTH - 1, 3):
            it.plus(c)
        for stage, ago in dma_waits:
            for c in range(2):
                it.plus16(1 - SKEW[stage] - ago + c)
        body(it)
        body(it.second())
    for i in range(graphs, graphs + DEPTH):
        body(Iteration(eng, graphs, number=i))


def gnn_stack(nc, x, adj, fc_w, fc_b, q_w, q_b, k_w, k_b, fp_w, fp_b,
              eps1, w11, b11, w12, b12, eps2, w21, b21, rms_w, w22, b22, w3, a3, out):
    B, N, D = x.shape
    NB = N // P
    assert D == P and NB == 2 and B % 2 == 0

    with ExitStack() as ctx:
        def sb(name, shape, dt=F32):
            return ctx.enter_context(nc.sbuf_tensor(name, shape, dt))

        def two(name, shape, dt=F32):
            return [sb(f"{name}_{p}", shape, dt) for p in range(2)]

        def bank(name):
            return ctx.enter_context(nc.psum_tensor(name, [P, 512], F32))

        attn_bank = [bank(f"attn_bank{k}") for k in range(NO)]
        val_bank = [bank(f"val_bank{k}") for k in range(2)]
        mid_bank = [bank(f"mid_bank{k}") for k in range(NMID)]

        ident = sb("ident", [P, P])
        self1 = sb("self1", [P, P])
        self2 = sb("self2", [P, P])
        minus_half = sb("minus_half", [P, 2])
        Wp = sb("Wp", [P, H0 * P])
        Wqk = sb("Wqk", [P, KROW + H0])
        qk_const = sb("qk_const", [KROW + H0, 1])
        bias0 = sb("bias0", [P, P])
        W11 = sb("W11", [P, HID1])
        B11 = sb("B11", [P, HID1 // P])
        W12 = sb("W12", [P, HID1 // P, P])
        B12 = sb("B12", [P, P])
        W21 = sb("W21", [P, HID2])
        B21 = sb("B21", [P, HID2])
        RMSW = sb("RMSW", [P, HID2])
        W22 = sb("W22", [P, HID2 // P, P])
        B22 = sb("B22", [P, P])
        W3 = sb("W3", [P, P])
        Wqk3 = sb("Wqk3", [P, KROW + H3])

        adjT = sb("adjT", [P, RING, NB, N], F16)
        limit = sb("limit", [P, RING, NB, N], BF16)

        x_in = two("x_in", [P, NB, P])
        adj_in = two("adj_in", [P, NB, N])
        xT = two("xT", [P, N])
        row_in = sb("row_in", [H0, N])
        row_exp = sb("row_exp", [H0, 2, N])
        row_R = two("row_R", [H0, N])
        kmax = sb("kmax", [KROW + H0, 1])
        kq = sb("kq", [H0, 1])
        nkmax = sb("nkmax", [KROW + H0, 2])
        E = two("E", [P, NB, 2, H0])
        nE = two("nE", [P, NB, H0])
        R = two("R", [P, H0, N])
        G = two("G", [P, NB, H0, GV])
        Wt = two("Wt", [P, NB, H0, N])
        x_bias = two("x_bias", [P, NB, P])
        x_twice = two("x_twice", [P, NB, P])
        rden = sb("rden", [P, NB, H0])
        T = two("T", [P, NB, H0, P])
        zsum = sb("zsum", [P, NB, P])
        sg0 = sb("sg0", [P, NB, P])
        y = {s: sb(f"y_{s}", [P, NB, P]) for s in "TCDF"}
        stats = {s: sb(f"stats_{s}", [P, NB, 6]) for s in "TCDF"}
        mv = {s: sb(f"mv_{s}", [P, NB, 2]) for s in "TCDF"}
        ve = {s: sb(f"ve_{s}", [P, NB]) for s in "TCDF"}
        rstd = {s: sb(f"rstd_{s}", [P, NB]) for s in "TCDF"}
        x1 = sb("x1", [P, NB, P])
        x1_hi, x1_lo = sb("x1_hi", [P, NB, P], F16), sb("x1_lo", [P, NB, P], F16)
        x1b = sb("x1b", [P, NB, P])
        agg1T = sb("agg1T", [P, N])
        hid1T = sb("hid1T", [P, HID1 // P, N])
        x2 = sb("x2", [P, NB, P])
        x2_hi, x2_lo = sb("x2_hi", [P, NB, P], F16), sb("x2_lo", [P, NB, P], F16)
        x2b = sb("x2b", [P, NB, P])
        agg2T = sb("agg2T", [P, N])
        hid2 = sb("hid2", [P, NB, HID2])
        sumsq = sb("sumsq", [P, NB])
        msq = sb("msq", [P, NB])
        rms = sb("rms", [P, NB])
        half_rms = sb("half_rms", [P, NB])
        gate = sb("gate", [P, NB, HID2])
        tanh2 = sb("tanh2", [P, NB, HID2])
        silT = sb("silT", [P, NB, HID2 // P, P])
        x3 = two("x3", [P, NB, P])
        x3T = two("x3T", [P, N])
        row3_in = sb("row3_in", [H3, N])
        row3_exp = sb("row3_exp", [H3, 2, N])
        row3_R = two("row3_R", [H3, N])
        kmax3 = sb("kmax3", [KROW + H3, 1])
        kq3 = sb("kq3", [H3, 1])
        nkmax3 = sb("nkmax3", [KROW + H3, 2])
        E3 = two("E3", [P, NB, 2, H3])
        nE3 = two("nE3", [P, NB, H3])
        R3 = two("R3", [P, H3, N])
        V3 = sb("V3", [P, NB, H3, HALF])
        Wt3 = sb("Wt3", [P, NB, H3, N])
        rden3 = sb("rden3", [P, NB, H3])
        out3T = sb("out3T", [P, 2 * N])
        out3 = sb("out3", [P, NB, P])
        x4 = two("x4", [P, NB, P])

        R_dram = nc.dram_tensor("R_dram", [2, H0, N], F32, kind="Internal").ap()
        R3_dram = nc.dram_tensor("R3_dram", [2, H3, N], F32, kind="Internal").ap()

        fcw = Wt[0][:, 0, 0:4, :].rearrange("p a n -> p (a n)")
        fpw = Wt[0][:, 0, 4:8, :].rearrange("p a (b e) -> p (a b) e", e=P)
        fcb = sb("fcb", [P, H0])
        qkw = sb("qkw", [P, 2])
        qkb = sb("qkb", [P, 2])
        fpb = sb("fpb", [P, P])
        eps = sb("eps", [P, 2])
        acol = sb("acol", [P, 2])
        ablk = sb("ablk", [P, 2, H3])
        fcwT = Wt[0][:, 1, 0:4, :].rearrange("p a (b e) -> p (a b) e", e=P)
        w3T = sb("w3T", [P, P])
        qk_sum = sb("qk_sum", [KROW + H0, 2])

        sig = Signals(lambda name: ctx.enter_context(nc.semaphore(name)))
        freed = sig.freed()
        ln = sig.ln
        FOLD_LOADS = [
            (fcw[:, :], fc_w), (qkw[:, 0:1], q_w), (qkw[:, 1:2], k_w), (W3[:, :], w3), (acol[:, :], a3),
            (fcb[:, :], fc_b), (qkb[:, 0:1], q_b.partition_broadcast(P)), (qkb[:, 1:2], k_b.partition_broadcast(P)),
        ]
        OTHER_LOADS = [
            (fpb[:, :], fp_b.partition_broadcast(P)),
            (eps[:, 0:1], eps1.partition_broadcast(P)), (eps[:, 1:2], eps2.partition_broadcast(P)),
            (W11[:, :], w11), (B11[:, :], b11),
            (W12[:, :, :], w12.rearrange("(c p) n -> p c n", p=P)), (B12[:, :], b12.partition_broadcast(P)),
            (W21[:, :], w21), (B21[:, :], b21.partition_broadcast(P)), (RMSW[:, :], rms_w.partition_broadcast(P)),
            (W22[:, :, :], w22.rearrange("(c p) n -> p c n", p=P)), (B22[:, :], b22.partition_broadcast(P)),
        ]
        CONSTANTS = 3

        with nc.Block() as block:
            @block.sync
            def _(sp):
                def fold_weights():
                    for dst, src in FOLD_LOADS:
                        sp.dma_start(dst, src).then_inc(sig.fold_loaded, 16)

                def other_weights():
                    sp.dma_start(fpw[:, :, :], fp_w.rearrange("(h j) e -> j h e", j=P)).then_inc(sig.fpw_loaded, 16)
                    for dst, src in OTHER_LOADS:
                        sp.dma_start(dst, src).then_inc(sig.weights_loaded, 16)

                def load(it):
                    g, p = it.graph("L"), it.parity("L")
                    if it.had("L", 2):
                        sp.wait_ge(sig.xT_done, it.done("L", 2))
                        sp.wait_ge(sig.xbias_ready, it.done("L", 2))
                    if it.had("L", 1):
                        sp.wait_ge(sig.x_loaded, it.dma_done("L", 1))
                        sp.wait_ge(sig.adj_loaded, it.dma_done("L", 1))
                    sp.dma_start(x_in[p][:, :, :],
                                 x[g].rearrange("(b p) d -> p b d", p=P)).then_inc(sig.x_loaded, 16)
                    if it.had("L", 2):
                        sp.wait_ge(sig.adjT_done, it.done("L", 2))
                    sp.dma_start(adj_in[p][:, :, :],
                                 adj[g].rearrange("(b p) m -> p b m", p=P)).then_inc(sig.adj_loaded, 16)

                def spread(it, stage, rows, dram, wide, ready, stored, loaded, used):
                    p = it.parity(stage)
                    sp.wait_ge(ready, it.done(stage))
                    sp.dma_start(dram[p], rows[p][:, :]).then_inc(stored, 16)
                    sp.wait_ge(stored, it.dma_done(stage))
                    if it.had(stage, 2):
                        sp.wait_ge(used, it.done(stage, 2))
                    sp.dma_start(wide[p][:, :, :], dram[p].partition_broadcast(P)).then_inc(loaded, 16)

                def store(it):
                    g, p = it.graph("S"), it.parity("S")
                    sp.wait_ge(ln["F"].norm, it.done("S"))
                    if it.had("S", 1):
                        sp.wait_ge(sig.out_stored, it.dma_done("S", 1))
                    sp.dma_start(out[g].rearrange("(b p) d -> p b d", p=P),
                                 x4[p][:, :, :]).then_inc(sig.out_stored, 16)

                def body(it):
                    l, a, e, s = (it.active(s) for s in "LAES")
                    if e:
                        spread(it, "E", row3_R, R3_dram, R3, sig.rowR3_ready, sig.R3_stored,
                               sig.R3_loaded, sig.edge3_done[1])
                    if l:
                        load(it)
                    if a:
                        spread(it, "A", row_R, R_dram, R, sig.rowR_ready, sig.R_stored,
                               sig.R_loaded, sig.edge_done[3])
                    if s:
                        store(it)
                    if it.number == SKEW["L"]:
                        other_weights()

                fold_weights()
                run_iterations(sp, B, body, [("L", 1), ("A", 0), ("E", 0), ("S", 1)])
                sp.wait_ge(sig.out_stored, 16 * B)
                sp.wait_ge(sig.R_loaded, 16 * B)
                sp.wait_ge(sig.R3_loaded, 16 * B)

            @block.tensor
            def _(pe):
                def fold_qk():
                    pe.wait_ge(sig.fold_loaded, 16 * len(FOLD_LOADS))
                    pe.wait_ge(sig.ident_ready, 1)
                    for h in range(H0):
                        pe.transpose(val_bank[h // 4][:, (h % 4) * P:(h % 4 + 1) * P],
                                     fcw[:, h * P:(h + 1) * P], ident[:, :])
                    pe.transpose(attn_bank[0][:, 0:P], W3[:, :], ident[:, :]).then_inc(sig.turned, 1)
                    pe.wait_ge(sig.turned_read, 1)
                    pe.wait_ge(sig.ablk_ready, 1)
                    for h in range(H0):
                        pe.matmul(attn_bank[1][:, 2 * h:2 * h + 2], fcwT[:, h, :], qkw[:, :],
                                  start=True, stop=True)
                    pe.matmul(val_bank[1][KROW:KROW + H0, 0:2], fcb[:, :], qkw[:, :], start=True, stop=True)
                    pe.matmul(attn_bank[0][:, 0:2 * H3], w3T[:, :], ablk[:, :, :].rearrange("p t h -> p (t h)"),
                              start=True, stop=True).then_inc(sig.qk_folded, 1)

                def fold_values():
                    pe.wait_ge(sig.qk_ready, 1)
                    pe.wait_ge(sig.fpw_loaded, 16)
                    for h in range(H0):
                        pe.matmul(attn_bank[h // 4][:, (h % 4) * P:(h % 4 + 1) * P], fcwT[:, h, :],
                                  fpw[:, h, :], start=True, stop=True)
                    for h in range(H0):
                        mm = pe.matmul(val_bank[0][:, 0:P], fcb[:, h:h + 1].broadcast_to([P, P]), fpw[:, h, :],
                                       start=h == 0, stop=h == H0 - 1)
                    mm.then_inc(sig.folded, 1)

                def mid(it, name):
                    k = INDEX[name]
                    back, j = 0, k
                    while it.number is None or back <= it.number:
                        j -= 1
                        if j < 0:
                            j, back = j + len(PHASES), back + 1
                        if j % NMID == k % NMID and it.active(PHASES[j][1], back):
                            if it.had(PHASES[j][1], back):
                                pe.wait_ge(freed[PHASES[j][0]], it.done(PHASES[j][1], back))
                            break
                    return mid_bank[k % NMID]

                def turn_x(it, name, src, written, value, done):
                    bank = mid(it, name)
                    pe.wait_ge(written, value)
                    for b in range(NB):
                        mm = pe.transpose(bank[:, b * P:(b + 1) * P], src[:, b, :], ident[:, :])
                    mm.then_inc(done, 1)

                def turn_adj(it):
                    bank, p = mid(it, "A_adjT"), it.parity("A")
                    pe.wait_ge(sig.adj_loaded, it.dma_done("A"))
                    for m in range(NB):
                        for n in range(NB):
                            mm = pe.transpose(bank[:, m * N + n * P:m * N + (n + 1) * P],
                                              adj_in[p][:, n, m * P:(m + 1) * P], ident[:, :])
                    mm.then_inc(sig.adjT_done, 1)

                def values(it, c):
                    m, half, p = c % 2, c // 2, it.parity("B")
                    if c == 0:
                        pe.wait_ge(sig.xT_ready, it.done("B"))
                    if c < 2:
                        if it.had("B", 1):
                            pe.wait_ge(sig.val_ready[c + 2], it.done("B", 1))
                    else:
                        pe.wait_ge(sig.val_ready[c - 2], it.done("B"))
                    pe.matmul(val_bank[c % 2][:, :], xT[p][:, m * P:(m + 1) * P],
                              Wp[:, 512 * half:512 * half + 512], start=True, stop=True).then_inc(sig.val_done[c], 1)

                def rows(it, name, stage, turned, w, ready, done):
                    bank, p = mid(it, name), it.parity(stage)
                    pe.wait_ge(ready, it.done(stage))
                    pe.matmul(bank[0:w.shape[1], 0:N], w[:, :], turned[p][:, :],
                              start=True, stop=True).then_inc(done, 1)

                def turn_E(it, name, stage, src, heads, ready, done):
                    pe.wait_ge(sig.ident_ready, 1)
                    bank = mid(it, name)
                    pe.wait_ge(ready, it.done(stage))
                    for b in range(NB):
                        for t in range(2):
                            k = (b * 2 + t) * heads
                            mm = pe.transpose(bank[:, k:k + heads], src[:, t, b * P:(b + 1) * P],
                                              ident[0:heads, 0:heads])
                    mm.then_inc(done, 1)

                def attend(it, u):
                    (g, n), p = UNITS[u], it.parity("P")
                    if u == 0:
                        for c in range(2):
                            pe.wait_ge(sig.weight_ready[c], it.done("P"))
                            pe.wait_ge(sig.val_ready[c], it.done("P"))
                    if u == 2:
                        for c in range(2, 4):
                            pe.wait_ge(sig.weight_ready[c], it.done("P"))
                            pe.wait_ge(sig.val_ready[c], it.done("P"))
                    if u < NO:
                        if it.had("P", 1):
                            pe.wait_ge(sig.attn_read[len(UNITS) - NO + u], it.done("P", 1))
                    else:
                        pe.wait_ge(sig.attn_read[u - NO], it.done("P"))
                    for h in range(*GROUPS[g]):
                        k = (h - GROUPS[g][0]) * GV
                        for m in range(NB):
                            mm = pe.matmul(attn_bank[u % NO][:, k:k + GV], Wt[p][:, m, h, n * P:(n + 1) * P],
                                           G[p][:, m, h, :], start=m == 0, stop=m == NB - 1)
                    mm.then_inc(sig.attn_done[u], 1)

                def aggregate(it, name, stage, xf, hi, lo, own, norm, split, done):
                    bank, g = mid(it, name), it.slot(stage)
                    pe.wait_ge(norm, it.done(stage))
                    pe.wait_ge(split, it.done(stage))
                    for k, part in enumerate((hi, lo)):
                        for m in range(NB):
                            pe.matmul(bank[:, 0:N], part[:, m, :], adjT[:, g, m, :],
                                      start=k == 0 and m == 0, stop=False)
                    for b in range(NB):
                        mm = pe.matmul(bank[:, b * P:(b + 1) * P], xf[:, b, :], own[:, :],
                                       start=False, stop=b == NB - 1)
                    mm.then_inc(done, 1)

                def hidden1(it):
                    bank = mid(it, "C_h")
                    pe.wait_ge(sig.agg1_ready, it.done("C"))
                    for j in range(HID1 // P):
                        mm = pe.matmul(bank[:, j * N:(j + 1) * N], W11[:, j * P:(j + 1) * P], agg1T[:, :],
                                       start=True, stop=True)
                    mm.then_inc(sig.hid1_done, 1)

                def project1(it):
                    bank = mid(it, "C_y")
                    pe.wait_ge(sig.hid1_ready, it.done("C"))
                    for b in range(NB):
                        for j in range(HID1 // P):
                            mm = pe.matmul(bank[:, b * P:(b + 1) * P], hid1T[:, j, b * P:(b + 1) * P],
                                           W12[:, j, :], start=j == 0, stop=j == HID1 // P - 1)
                    mm.then_inc(sig.y1_done, 1)

                def hidden2(it, b):
                    bank = mid(it, f"D_h{b}")
                    pe.wait_ge(sig.agg2_ready, it.done("D"))
                    pe.matmul(bank[:, :], agg2T[:, b * P:(b + 1) * P], W21[:, :],
                              start=True, stop=True).then_inc(sig.hid2_done[b], 1)

                def turn_sil(it, b):
                    bank = mid(it, f"D_t{b}")
                    pe.wait_ge(sig.sil_done[b], it.done("D"))
                    for j in range(HID2 // P):
                        mm = pe.transpose(bank[:, j * P:(j + 1) * P], tanh2[:, b, j * P:(j + 1) * P], ident[:, :])
                    mm.then_inc(sig.silT_done[b], 1)

                def project2(it):
                    bank = mid(it, "D_y")
                    for b in range(NB):
                        pe.wait_ge(sig.silT_ready[b], it.done("D"))
                        for j in range(HID2 // P):
                            mm = pe.matmul(bank[:, b * P:(b + 1) * P], silT[:, b, j, :], W22[:, j, :],
                                           start=j == 0, stop=j == HID2 // P - 1)
                    mm.then_inc(sig.y2_done, 1)

                def values3(it):
                    bank, p = mid(it, "F_V"), it.parity("F")
                    pe.wait_ge(sig.x3T_ready, it.done("F"))
                    for m in range(NB):
                        mm = pe.matmul(bank[:, m * P:(m + 1) * P], x3T[p][:, m * P:(m + 1) * P], W3[:, :],
                                       start=True, stop=True)
                    mm.then_inc(sig.V3_done, 1)

                def attend3(it):
                    bank = mid(it, "F_O")
                    pe.wait_ge(sig.V3_ready, it.done("F"))
                    for m in range(NB):
                        pe.wait_ge(sig.weight3_ready[m], it.done("F"))
                    for k in range(2):
                        for m in range(NB):
                            for half in range(2):
                                mm = pe.matmul(bank[half * HALF:(half + 1) * HALF, k * N:(k + 1) * N],
                                               V3[:, m, 2 * k + half, :], Wt3[:, m, 2 * k + half, :],
                                               start=m == 0, stop=m == NB - 1)
                    mm.then_inc(sig.out3T_done, 1)

                def turn_out3(it):
                    pe.wait_ge(sig.ident_ready, 1)
                    bank = mid(it, "F_T")
                    pe.wait_ge(sig.out3T_ready, it.done("F"))
                    for n in range(NB):
                        for k in range(H3 // 2):
                            c = n * H3 * HALF + k * P
                            mm = pe.transpose(bank[:, c:c + P], out3T[:, k * N + n * P:k * N + (n + 1) * P],
                                              ident[:, :])
                    mm.then_inc(sig.out3_done, 1)

                def body(it):
                    a, b, p, c, d, e, f = (it.active(s) for s in "ABPCDEF")
                    if it.number == SKEW["A"]:
                        pe.wait_ge(sig.qk_ready, 1)
                    if it.number == SKEW["B"]:
                        pe.wait_ge(sig.constants_ready, CONSTANTS)
                        pe.wait_ge(sig.weights_loaded, 16 * len(OTHER_LOADS))
                    if p:
                        attend(it, 0)
                    if b:
                        values(it, 0)
                    if a:
                        turn_x(it, "A_xT", x_in[it.parity("A")],
                               sig.x_loaded, it.dma_done("A"), sig.xT_done)
                    if b:
                        values(it, 1)
                    if a:
                        turn_adj(it)
                    if d:
                        aggregate(it, "D_agg", "D", x2, x2_hi, x2_lo, self2, ln["C"].norm, sig.x2_split,
                                  sig.agg2_done)
                    if p:
                        attend(it, 1)
                    if d:
                        hidden2(it, 0)
                        hidden2(it, 1)
                    if e:
                        turn_x(it, "E_xT", x3[it.parity("E")],
                               ln["D"].norm, it.done("E"), sig.x3T_done)
                    if b:
                        values(it, 2)
                    if f:
                        values3(it)
                    if a:
                        rows(it, "A_rows", "A", xT, Wqk, sig.xT_ready, sig.rows_done)
                    if p:
                        attend(it, 2)
                    if e:
                        rows(it, "E_rows", "E", x3T, Wqk3, sig.x3T_ready, sig.rows3_done)
                    if f:
                        attend3(it)
                    if p:
                        attend(it, 3)
                    if b:
                        values(it, 3)
                    if a:
                        turn_E(it, "A_E", "A", row_exp, H0, sig.rowE_ready, sig.E_done)
                    if c:
                        aggregate(it, "C_agg", "C", x1, x1_hi, x1_lo, self1, ln["T"].norm, sig.x1_split,
                                  sig.agg1_done)
                    if d:
                        turn_sil(it, 0)
                    if f:
                        turn_out3(it)
                    if c:
                        hidden1(it)
                    if p:
                        attend(it, 4)
                    if d:
                        turn_sil(it, 1)
                    if c:
                        project1(it)
                    if e:
                        turn_E(it, "E_E", "E", row3_exp, H3, sig.rowE3_ready, sig.E3_done)
                    if d:
                        project2(it)
                    if p:
                        attend(it, 5)
                    if it.number == SKEW["A"]:
                        fold_values()

                fold_qk()
                run_iterations(pe, B, body, [("A", 0)])

            @block.scalar
            def _(act):
                def turned_weights():
                    act.wait_ge(sig.turned, 1)
                    for half in range(2):
                        nc.scalar.copy(fcwT[:, 4 * half:4 * half + 4, :].rearrange("p h j -> p (h j)"),
                                       val_bank[half][:, :])
                    nc.scalar.copy(w3T[:, :], attn_bank[0][:, 0:P]).then_inc(sig.turned_read, 1)

                def value_weights():
                    act.wait_ge(sig.folded, 1)
                    for half in range(2):
                        nc.scalar.copy(Wp[:, 512 * half:512 * half + 512],
                                       attn_bank[half][:, :]).then_inc(sig.constants_ready, 1)

                def copy_out(it, stage, done, dst, src, ready):
                    act.wait_ge(done, it.done(stage))
                    nc.scalar.copy(dst, src).then_inc(ready, 1)

                def bank(name):
                    return mid_bank[INDEX[name] % NMID]

                def values(it, c):
                    m, half, p = c % 2, c // 2, it.parity("B")
                    act.wait_ge(sig.val_done[c], it.done("B"))
                    nc.scalar.copy(G[p][:, m, 4 * half:4 * half + 4, 0:P],
                                   val_bank[c % 2][:, :].rearrange("p (h e) -> p h e", e=P)
                                   ).then_inc(sig.val_ready[c], 1)

                def exponentials(it, name, stage, slope, row, nkmax, heads, row_R, row_E, read, stored, ready, E_ready):
                    p = it.parity(stage)
                    keys = slice(KROW, KROW + heads)
                    act.wait_ge(read, it.done(stage))
                    if it.had(stage, 2):
                        act.wait_ge(stored, it.dma_done(stage, 2))
                    nc.scalar.activation(row_R[p][:, :], row[:, :], ACT.Exp, scale=1.0 - slope).then_inc(ready, 1)
                    nc.scalar.activation(row_E[:, 0, :], bank(name)[keys, 0:N], ACT.Exp, bias=nkmax[keys, 0:1])
                    nc.scalar.activation(row_E[:, 1, :], bank(name)[keys, 0:N], ACT.Exp, bias=nkmax[keys, 1:2],
                                         scale=slope).then_inc(E_ready, 1)

                def relu1(it):
                    act.wait_ge(sig.hid1_done, it.done("C"))
                    for j in range(HID1 // P):
                        last = nc.scalar.activation(hid1T[:, j, :], bank("C_h")[:, j * N:(j + 1) * N],
                                                    ACT.Relu, bias=B11[:, j:j + 1])
                    last.then_inc(sig.hid1_ready, 1)

                def squares(it, b):
                    act.wait_ge(sig.hid2_ready[b], it.done("D"))
                    if it.had("D", 1):
                        act.wait_ge(sig.silT_done[b], it.done("D", 1))
                    nc.scalar.activation(tanh2[:, b, :], hid2[:, b, :], ACT.Square,
                                         accum_out=sumsq[:, b:b + 1]).then_inc(sig.sumsq_done[b], 1)

                def edges(it, c):
                    m, half, p = c % 2, c // 2, it.parity("B")
                    act.wait_ge(sig.R_loaded, it.dma_done("B"))
                    act.wait_ge(sig.E_ready, it.done("B"))
                    if it.had("B", 2):
                        act.wait_ge(sig.attn_done[5], it.done("B", 2))
                    for h in range(4 * half, 4 * half + 4):
                        last = nc.scalar.activation(Wt[p][:, m, h, :], R[p][:, h, :], ACT.Relu,
                                                    scale=E[p][:, m, 0, h:h + 1], bias=nE[p][:, m, h:h + 1])
                    last.then_inc(sig.edge_done[c], 1)

                def edges3(it, m):
                    p = it.parity("F")
                    act.wait_ge(sig.R3_loaded, it.dma_done("F"))
                    act.wait_ge(sig.E3_ready, it.done("F"))
                    if it.had("F", 1):
                        act.wait_ge(sig.out3T_done, it.done("F", 1))
                    for h in range(H3):
                        last = nc.scalar.activation(Wt3[:, m, h, :], R3[p][:, h, :], ACT.Relu,
                                                    scale=E3[p][:, m, 0, h:h + 1], bias=nE3[p][:, m, h:h + 1])
                    last.then_inc(sig.edge3_done[m], 1)

                def columns(it, stage, name, E, nE, heads, turned, ready):
                    p = it.parity(stage)
                    act.wait_ge(turned, it.done(stage))
                    src = bank(name)[:, 0:NB * 2 * heads].rearrange("p (b t h) -> p b t h", b=NB, t=2)
                    nc.scalar.copy(E[p][:, :, :, :], src)
                    nc.scalar.mul(nE[p][:, :, :], src[:, :, 1, :], -1.0).then_inc(ready, 1)

                def tanhs(it, b):
                    act.wait_ge(sig.half_done, it.done("D"))
                    act.wait_ge(sig.gate_done[b], it.done("D"))
                    nc.scalar.activation(tanh2[:, b, :], gate[:, b, :], ACT.Tanh,
                                         scale=half_rms[:, b:b + 1]).then_inc(sig.tanh_done[b], 1)

                def tanh0(it):
                    act.wait_ge(sig.zsum_ready, it.done("C"))
                    nc.scalar.activation(sg0[:, :, :], zsum[:, :, :], ACT.Tanh, scale=0.5).then_inc(sig.sg0_ready, 1)

                def body(it):
                    a, b, c, d, e, f = (it.active(s) for s in "ABCDEF")
                    if it.number == SKEW["B"]:
                        value_weights()
                        act.wait_ge(sig.weights_loaded, 16 * len(OTHER_LOADS))
                    if f:
                        edges3(it, 1)
                        edges3(it, 0)
                    if d:
                        copy_out(it, "D", sig.agg2_done, agg2T[:, :], bank("D_agg")[:, 0:N], sig.agg2_ready)
                    if a:
                        copy_out(it, "A", sig.xT_done, xT[it.parity("A")][:, :], bank("A_xT")[:, 0:N], sig.xT_ready)
                    if b:
                        values(it, 0)
                    if a:
                        copy_out(it, "A", sig.adjT_done,
                                 adjT[:, it.slot("A"), :, :],
                                 bank("A_adjT")[:, :].rearrange("p (m n) -> p m n", m=NB), sig.adjT_ready)
                    if b:
                        edges(it, 1)
                    if c:
                        tanh0(it)
                    if d:
                        squares(it, 0)
                        squares(it, 1)
                    if e:
                        copy_out(it, "E", sig.x3T_done, x3T[it.parity("E")][:, :], bank("E_xT")[:, 0:N],
                                 sig.x3T_ready)
                    if f:
                        copy_out(it, "F", sig.V3_done, V3[:, :, :, 0:D3],
                                 bank("F_V")[:, 0:N].rearrange("p (m h e) -> p m h e", m=NB, h=H3), sig.V3_ready)
                    if b:
                        edges(it, 0)
                        values(it, 1)
                    if d:
                        tanhs(it, 0)
                    if a:
                        exponentials(it, "A_rows", "A", A0, row_in, nkmax, H0, row_R, row_exp, sig.rows_read, sig.R_stored,
                                     sig.rowR_ready, sig.rowE_ready)
                    if e:
                        exponentials(it, "E_rows", "E", A3, row3_in, nkmax3, H3, row3_R, row3_exp, sig.rows3_read, sig.R3_stored,
                                     sig.rowR3_ready, sig.rowE3_ready)
                    if a:
                        columns(it, "A", "A_E", E, nE, H0, sig.E_done, sig.E_ready)
                    if f:
                        copy_out(it, "F", sig.out3T_done, out3T[:, :], bank("F_O")[:, :], sig.out3T_ready)
                    if c:
                        copy_out(it, "C", sig.agg1_done, agg1T[:, :], bank("C_agg")[:, 0:N], sig.agg1_ready)
                    if d:
                        tanhs(it, 1)
                    if b:
                        values(it, 2)
                    if d:
                        copy_out(it, "D", sig.silT_done[0], silT[:, 0, :, :].rearrange("p j n -> p (j n)"),
                                 bank("D_t0")[:, :], sig.silT_ready[0])
                    if c:
                        relu1(it)
                    if b:
                        values(it, 3)
                    if d:
                        copy_out(it, "D", sig.silT_done[1], silT[:, 1, :, :].rearrange("p j n -> p (j n)"),
                                 bank("D_t1")[:, :], sig.silT_ready[1])
                    if b:
                        edges(it, 2)
                    if e:
                        columns(it, "E", "E_E", E3, nE3, H3, sig.E3_done, sig.E3_ready)
                    if b:
                        edges(it, 3)

                turned_weights()
                run_iterations(act, B, body, [("A", 2), ("E", 2), ("B", 0), ("F", 0)])

            @block.vector
            def _(dve):
                def qk_weights():
                    nc.vector.memset(minus_half[:, :], -0.5)
                    for p in range(2):
                        nc.vector.memset(G[p][:, :, :, P:GV], 1.0)
                    nc.vector.memset(V3[:, :, :, D3:HALF], 0.0).then_inc(sig.zeroed, 1)
                    dve.wait_ge(sig.zeroed, 1)
                    nc.vector.memset(V3[:, :, :, D3:D3 + 1], 1.0)
                    nc.vector.memset(Wqk[:, :], 0.0)
                    nc.vector.memset(Wqk3[:, :], 0.0)
                    nc.vector.memset(ablk[:, :, :], 0.0).then_inc(sig.zeroed, 1)
                    dve.wait_ge(sig.zeroed, 2)
                    dve.wait_ge(sig.fold_loaded, 16 * len(FOLD_LOADS))
                    for h in range(H3):
                        last = nc.vector.tensor_copy(ablk[h * D3:(h + 1) * D3, :, h],
                                                     acol[h * D3:(h + 1) * D3, :])
                    last.then_inc(sig.ablk_ready, 1)
                    dve.wait_ge(sig.qk_folded, 1)
                    qk = attn_bank[1][:, 0:2 * H0].rearrange("p (h t) -> p t h", t=2)
                    for t in range(2):
                        nc.vector.tensor_copy(Wqk[:, t * KROW:t * KROW + H0], qk[:, t, :])
                        nc.vector.tensor_copy(Wqk3[:, t * KROW:t * KROW + H3],
                                              attn_bank[0][:, t * H3:(t + 1) * H3])
                    nc.vector.tensor_tensor(qk_sum[KROW:KROW + H0, :], val_bank[1][KROW:KROW + H0, 0:2],
                                            qkb[KROW:KROW + H0, :], ALU.add).then_inc(sig.qk_summed, 1)
                    dve.wait_ge(sig.qk_summed, 1)
                    nc.vector.reduce_sum(qk_const[KROW:KROW + H0, :], qk_sum[KROW:KROW + H0, :],
                                         AX.X).then_inc(sig.qk_ready, 1)

                def other_constants():
                    dve.wait_ge(sig.folded, 1)
                    dve.wait_ge(sig.weights_loaded, 16 * len(OTHER_LOADS))
                    nc.vector.tensor_tensor(bias0[:, :], val_bank[0][:, 0:P], fpb[:, :], ALU.add)
                    nc.vector.scalar_tensor_tensor(out=self1[:, :], in0=ident[:, :], scalar=eps[:, 0:1],
                                                   in1=ident[:, :], op0=ALU.mult, op1=ALU.add)
                    nc.vector.tensor_scalar(self2[:, :], ident[:, :], eps[:, 1:2], None,
                                            ALU.mult).then_inc(sig.constants_ready, 1)

                def bank(name):
                    return mid_bank[INDEX[name] % NMID]

                def limits(it):
                    g = it.slot("A")
                    dve.wait_ge(sig.adjT_ready, it.done("A"))
                    nc.vector.tensor_scalar(limit[:, g, :, :], adjT[:, g, :, :], BIG, FLOOR,
                                            ALU.mult, ALU.add).then_inc(sig.limit_ready, 1)

                def key_maximum(it, name, stage, heads, kmax, done, max_done):
                    keys = slice(KROW, KROW + heads)
                    dve.wait_ge(done, it.done(stage))
                    nc.vector.reduce_max(kmax[keys, 0:1], bank(name)[keys, 0:N], AX.X).then_inc(max_done, 1)

                def key_constants(it, stage, heads, slope, const, kmax, nkmax, kq, max_done, kq_done):
                    keys = slice(KROW, KROW + heads)
                    dve.wait_ge(max_done, it.done(stage))
                    nc.vector.tensor_scalar(nkmax[keys, 0:1], kmax[keys, 0:1], -1.0, None, ALU.mult)
                    nc.vector.tensor_scalar(nkmax[keys, 1:2], kmax[keys, 0:1], -slope, None, ALU.mult)
                    nc.vector.tensor_scalar(kq[:, 0:1], kmax[keys, 0:1], const, None, ALU.add).then_inc(kq_done, 1)

                def query_rows(it, name, stage, heads, slope, row, kq, kq_done, read):
                    dve.wait_ge(kq_done, it.done(stage))
                    nc.vector.tensor_scalar(row[:, :], bank(name)[0:heads, 0:N], kq[:, 0:1], CLAMP / (1 - slope),
                                            ALU.add, ALU.min).then_inc(read, 1)

                def weights(it, c):
                    m, half, p, g = c % 2, c // 2, it.parity("B"), it.slot("B")
                    dve.wait_ge(sig.limit_ready, it.done("B"))
                    dve.wait_ge(sig.E_ready, it.done("B"))
                    dve.wait_ge(sig.edge_done[c], it.done("B"))
                    for h in range(4 * half, 4 * half + 4):
                        w = Wt[p][:, m, h, :]
                        last = nc.vector.scalar_tensor_tensor(out=w, in0=w, scalar=E[p][:, m, 1, h:h + 1],
                                                              in1=limit[:, g, m, :], op0=ALU.add, op1=ALU.min)
                    last.then_inc(sig.weight_ready[c], 1)

                def weights3(it, m):
                    p, g = it.parity("F"), it.slot("F")
                    dve.wait_ge(sig.E3_ready, it.done("F"))
                    dve.wait_ge(sig.edge3_done[m], it.done("F"))
                    for h in range(H3):
                        last = nc.vector.scalar_tensor_tensor(
                            out=Wt3[:, m, h, :], in0=Wt3[:, m, h, :], scalar=E3[p][:, m, 1, h:h + 1],
                            in1=limit[:, g, m, :], op0=ALU.add, op1=ALU.min)
                    last.then_inc(sig.weight3_ready[m], 1)

                def products(u):
                    heads = GROUPS[UNITS[u][0]]
                    return attn_bank[u % NO][:, 0:(heads[1] - heads[0]) * GV].rearrange("p (h e) -> p h e", e=GV)

                def reciprocals(it, u):
                    (g, n), p = UNITS[u], it.parity("P")
                    dve.wait_ge(sig.attn_done[u], it.done("P"))
                    nc.vector.reciprocal(rden[:, n, slice(*GROUPS[g])], products(u)[:, :, P]).then_inc(sig.attn_sum[u], 1)

                def normalise(it, u):
                    (g, n), p = UNITS[u], it.parity("P")
                    lo, hi = GROUPS[g]
                    if u == 0:
                        if it.had("P", 2):
                            dve.wait_ge(sig.zsum_ready, it.done("P", 2))
                    dve.wait_ge(sig.attn_sum[u], it.done("P"))
                    nc.vector.tensor_tensor(T[p][:, n, lo:hi, :], products(u)[:, :, 0:P],
                                            rden[:, n, lo:hi].unsqueeze(2).broadcast_to([P, hi - lo, P]),
                                            ALU.mult).then_inc(sig.attn_read[u], 1)

                def statistics(it, s, stage):
                    dve.wait_ge(ln[s].y, it.done(stage))
                    for b in range(NB):
                        last = nc.vector.bn_stats(stats[s][:, b, :], y[s][:, b, :])
                    last.then_inc(ln[s].stats, 1)

                def moments(it, s, stage):
                    dve.wait_ge(sig.ident_ready, 1)
                    dve.wait_ge(ln[s].stats, it.done(stage))
                    for b in range(NB):
                        last = nc.vector.bn_aggr(mv[s][:, b, :], stats[s][:, b, :])
                    last.then_inc(ln[s].mv, 1)

                def norm(it, s, stage, dst):
                    dve.wait_ge(ln[s].rstd, it.done(stage))
                    for b in range(NB):
                        last = nc.vector.tensor_scalar(dst[:, b, :], y[s][:, b, :], mv[s][:, b, 0:1],
                                                       rstd[s][:, b:b + 1], ALU.subtract, ALU.mult)
                    last.then_inc(ln[s].norm, 1)

                def residual1(it):
                    dve.wait_ge(sig.y1_done, it.done("C"))
                    dve.wait_ge(sig.x1b_ready, it.done("C"))
                    if it.had("C", 1):
                        dve.wait_ge(ln["C"].norm, it.done("C", 1))
                    nc.vector.tensor_tensor(y["C"][:, :, :],
                                            bank("C_y")[:, 0:N].rearrange("p (b e) -> p b e", b=NB),
                                            x1b[:, :, :], ALU.add).then_inc(ln["C"].y, 1)

                def bias2(it, b):
                    dve.wait_ge(sig.hid2_done[b], it.done("D"))
                    if it.had("D", 1):
                        dve.wait_ge(sig.gate_done[b], it.done("D", 1))
                        dve.wait_ge(sig.sumsq_done[b], it.done("D", 1))
                    nc.vector.tensor_tensor(hid2[:, b, :], bank(f"D_h{b}")[:, :], B21[:, :],
                                            ALU.add).then_inc(sig.hid2_ready[b], 1)

                def silu2(it, b):
                    dve.wait_ge(sig.tanh_done[b], it.done("D"))
                    nc.vector.scalar_tensor_tensor(out=tanh2[:, b, :], in0=tanh2[:, b, :], scalar=1.0,
                                                   in1=gate[:, b, :], op0=ALU.add,
                                                   op1=ALU.mult).then_inc(sig.sil_done[b], 1)

                def residual2(it):
                    dve.wait_ge(sig.y2_done, it.done("D"))
                    dve.wait_ge(sig.x2b_ready, it.done("D"))
                    if it.had("D", 1):
                        dve.wait_ge(ln["D"].norm, it.done("D", 1))
                    for b in range(NB):
                        last = nc.vector.scalar_tensor_tensor(
                            out=y["D"][:, b, :], in0=bank("D_y")[:, b * P:(b + 1) * P],
                            scalar=half_rms[:, b:b + 1], in1=x2b[:, b, :], op0=ALU.mult, op1=ALU.add)
                    last.then_inc(ln["D"].y, 1)

                def products3():
                    return bank("F_T")[:, :].rearrange("p (k e) -> p k e", e=HALF)

                def reciprocals3(it):
                    dve.wait_ge(sig.out3_done, it.done("F"))
                    nc.vector.reciprocal(rden3[:, :, :].rearrange("p b h -> p (b h)"),
                                         products3()[:, :, D3]).then_inc(sig.sum3_done, 1)

                def normalise3(it):
                    dve.wait_ge(sig.sum3_done, it.done("F"))
                    if it.had("F", 1):
                        dve.wait_ge(ln["F"].y, it.done("F", 1))
                    nc.vector.tensor_tensor(
                        out3[:, :, :].rearrange("p b (h e) -> p (b h) e", h=H3), products3()[:, :, 0:D3],
                        rden3[:, :, :].rearrange("p b h -> p (b h)").unsqueeze(2).broadcast_to([P, NB * H3, D3]),
                        ALU.mult).then_inc(sig.out3_read, 1)

                def body(it):
                    a, b, p, c, d, e, f = (it.active(s) for s in "ABPCDEF")
                    if it.number == SKEW["A"]:
                        dve.wait_ge(sig.qk_ready, 1)
                    if it.number == SKEW["B"]:
                        other_constants()
                    if f:
                        weights3(it, 1)
                    if p:
                        reciprocals(it, 0)
                    if d:
                        bias2(it, 0)
                    if p:
                        normalise(it, 0)
                    if d:
                        bias2(it, 1)
                    if f:
                        weights3(it, 0)
                    if c:
                        statistics(it, "T", "C")
                    if p:
                        reciprocals(it, 1)
                    if c:
                        moments(it, "T", "C")
                    if a:
                        key_maximum(it, "A_rows", "A", H0, kmax, sig.rows_done, sig.kmax_done)
                    if p:
                        normalise(it, 1)
                    if e:
                        key_maximum(it, "E_rows", "E", H3, kmax3, sig.rows3_done, sig.kmax3_done)
                    if a:
                        key_constants(it, "A", H0, A0, qk_const[KROW:KROW + H0, 0:1], kmax, nkmax, kq,
                                      sig.kmax_done, sig.kq_done)
                    if c:
                        if it.had("C", 1):
                            dve.wait_ge(sig.agg1_done, it.done("C", 1))
                            dve.wait_ge(sig.x1b_ready, it.done("C", 1))
                        norm(it, "T", "C", x1)
                    if a:
                        query_rows(it, "A_rows", "A", H0, A0, row_in, kq, sig.kq_done, sig.rows_read)
                    if p:
                        reciprocals(it, 2)
                    if e:
                        key_constants(it, "E", H3, A3, 0.0, kmax3, nkmax3, kq3, sig.kmax3_done, sig.kq3_done)
                    if p:
                        normalise(it, 2)
                    if e:
                        query_rows(it, "E_rows", "E", H3, A3, row3_in, kq3, sig.kq3_done, sig.rows3_read)
                    if p:
                        reciprocals(it, 3)
                    if d:
                        silu2(it, 0)
                    if p:
                        normalise(it, 3)
                    if b:
                        weights(it, 0)
                    if f:
                        reciprocals3(it)
                    if d:
                        silu2(it, 1)
                    if f:
                        normalise3(it)
                    if b:
                        weights(it, 1)
                    if f:
                        statistics(it, "F", "F")
                    if c:
                        residual1(it)
                    if p:
                        reciprocals(it, 4)
                    if c:
                        statistics(it, "C", "C")
                        moments(it, "C", "C")
                    if a:
                        limits(it)
                    if p:
                        normalise(it, 4)
                    if f:
                        moments(it, "F", "F")
                    if d:
                        residual2(it)
                    if c:
                        if it.had("C", 1):
                            dve.wait_ge(sig.agg2_done, it.done("C", 1))
                            dve.wait_ge(sig.x2b_ready, it.done("C", 1))
                        norm(it, "C", "C", x2)
                    if p:
                        reciprocals(it, 5)
                    if d:
                        statistics(it, "D", "D")
                    if p:
                        normalise(it, 5)
                    if d:
                        moments(it, "D", "D")
                    if b:
                        weights(it, 2)
                        weights(it, 3)
                    if f:
                        if it.had("F", 2):
                            dve.wait_ge(sig.out_stored, it.dma_done("F", 2))
                        norm(it, "F", "F", x4[it.parity("F")])
                    if d:
                        if it.had("D", 2):
                            dve.wait_ge(ln["F"].y, it.done("D", 2))
                        norm(it, "D", "D", x3[it.parity("D")])

                qk_weights()
                run_iterations(dve, B, body, [("F", 2)])

            @block.gpsimd
            def _(pool):
                def identity():
                    nc.gpsimd.memset(ident[:, :], 0.0).then_inc(sig.ident_zero, 1)
                    pool.wait_ge(sig.ident_zero, 1)
                    nc.gpsimd.affine_select(out=ident[:, :], in_=ident[:, :], compare_op=ALU.not_equal,
                                            fill=1.0, base=0, pattern=[[-1, P]],
                                            channel_multiplier=1).then_inc(sig.ident_ready, 1)

                def head_sum(it, heads, before, done):
                    t, half = T[it.parity("C")], heads // 2
                    pool.wait_ge(before, it.done("C"))
                    nc.gpsimd.tensor_tensor(t[:, :, 0:half, :], t[:, :, 0:half, :], t[:, :, half:heads, :],
                                            ALU.add).then_inc(done, 1)

                def residual_sum(it):
                    p = it.parity("C")
                    pool.wait_ge(sig.tree3_done, it.done("C"))
                    nc.gpsimd.tensor_tensor(zsum[:, :, :], T[p][:, :, 0, :], x_bias[p][:, :, :],
                                            ALU.add).then_inc(sig.zsum_ready, 1)

                def residual0(it):
                    pool.wait_ge(sig.sg0_ready, it.done("C"))
                    nc.gpsimd.tensor_tensor(y["T"][:, :, :], sg0[:, :, :], x_twice[it.parity("C")][:, :, :],
                                            ALU.add).then_inc(ln["T"].y, 1)

                def residual3(it):
                    pool.wait_ge(sig.out3_read, it.done("F"))
                    if it.had("F", 1):
                        pool.wait_ge(ln["F"].norm, it.done("F", 1))
                    nc.gpsimd.tensor_tensor(y["F"][:, :, :], out3[:, :, :], x3[it.parity("F")][:, :, :],
                                            ALU.add).then_inc(ln["F"].y, 1)

                def x_terms(it):
                    p = it.parity("B")
                    pool.wait_ge(sig.ident_ready, 1)
                    if it.had("B", 2):
                        pool.wait_ge(ln["T"].y, it.done("B", 2))
                    pool.wait_ge(sig.x_loaded, it.dma_done("B"))
                    nc.gpsimd.tensor_scalar(x_twice[p][:, :, :], x_in[p][:, :, :], 2.0, 1.0, ALU.mult, ALU.add)
                    nc.gpsimd.tensor_tensor(x_bias[p][:, :, :], x_in[p][:, :, :],
                                            bias0[:, :].unsqueeze(1).broadcast_to([P, NB, P]),
                                            ALU.add).then_inc(sig.xbias_ready, 1)

                def rsqrt_var(it, s, stage):
                    pool.wait_ge(sig.ident_ready, 1)
                    pool.wait_ge(ln[s].mv, it.done(stage))
                    nc.gpsimd.tensor_scalar(ve[s][:, :], mv[s][:, :, 1], EPS[s], 1.0, ALU.add,
                                            ALU.mult).then_inc(ln[s].ve, 1)
                    pool.wait_ge(ln[s].ve, it.done(stage))
                    nc.gpsimd.tensor_tensor(rstd[s][:, :], ve[s][:, :], minus_half[:, :],
                                            ALU.pow).then_inc(ln[s].rstd, 1)

                def split(it, stage, src, hi, lo, agg_done, norm_done, hi_done, done):
                    pool.wait_ge(sig.ident_ready, 1)
                    pool.wait_ge(norm_done, it.done(stage))
                    if it.had(stage, 1):
                        pool.wait_ge(agg_done, it.done(stage, 1))
                    nc.gpsimd.tensor_copy(hi[:, :, :], src[:, :, :]).then_inc(hi_done, 1)
                    pool.wait_ge(hi_done, it.done(stage))
                    nc.gpsimd.tensor_tensor(lo[:, :, :], src[:, :, :], hi[:, :, :], ALU.subtract).then_inc(done, 1)

                def add_bias(it, stage, dst, src, bias, written, y_done, done):
                    pool.wait_ge(written, it.done(stage))
                    if it.had(stage, 1):
                        pool.wait_ge(y_done, it.done(stage, 1))
                    nc.gpsimd.tensor_tensor(dst[:, :, :], src[:, :, :],
                                            bias[:, :].unsqueeze(1).broadcast_to([P, NB, P]),
                                            ALU.add).then_inc(done, 1)

                def gates(it, b):
                    pool.wait_ge(sig.hid2_ready[b], it.done("D"))
                    if it.had("D", 1):
                        pool.wait_ge(sig.sil_done[b], it.done("D", 1))
                    nc.gpsimd.tensor_tensor(gate[:, b, :], hid2[:, b, :], RMSW[:, :],
                                            ALU.mult).then_inc(sig.gate_done[b], 1)

                def rsqrt_rms(it):
                    pool.wait_ge(sig.ident_ready, 1)
                    if it.had("D", 1):
                        pool.wait_ge(ln["D"].y, it.done("D", 1))
                    for b in range(NB):
                        pool.wait_ge(sig.sumsq_done[b], it.done("D"))
                    nc.gpsimd.tensor_scalar(msq[:, :], sumsq[:, :], 1.0 / HID2, RMS_EPS, ALU.mult,
                                            ALU.add).then_inc(sig.msq_done, 1)
                    pool.wait_ge(sig.msq_done, it.done("D"))
                    nc.gpsimd.tensor_tensor(rms[:, :], msq[:, :], minus_half[:, :],
                                            ALU.pow).then_inc(sig.rms_done, 1)
                    pool.wait_ge(sig.ident_ready, 1)
                    pool.wait_ge(sig.rms_done, it.done("D"))
                    nc.gpsimd.tensor_scalar(half_rms[:, :], rms[:, :], 0.5, 1.0, ALU.mult,
                                            ALU.mult).then_inc(sig.half_done, 1)

                def body(it):
                    b, c, d, f = (it.active(s) for s in "BCDF")
                    if it.number == SKEW["B"]:
                        pool.wait_ge(sig.constants_ready, CONSTANTS)
                        pool.wait_ge(sig.weights_loaded, 16 * len(OTHER_LOADS))
                    if c:
                        head_sum(it, 8, sig.attn_read[5], sig.tree1_done)
                        head_sum(it, 4, sig.tree1_done, sig.tree2_done)
                        head_sum(it, 2, sig.tree2_done, sig.tree3_done)
                        residual_sum(it)
                    if d:
                        gates(it, 0)
                    if c:
                        residual0(it)
                    if d:
                        rsqrt_rms(it)
                    if c:
                        rsqrt_var(it, "T", "C")
                        split(it, "C", x1, x1_hi, x1_lo, sig.agg1_done, ln["T"].norm, sig.x1_hi_done, sig.x1_split)
                    if d:
                        gates(it, 1)
                    if c:
                        add_bias(it, "C", x1b, x1, B12, ln["T"].norm, ln["C"].y, sig.x1b_ready)
                    if b:
                        x_terms(it)
                    if d:
                        add_bias(it, "D", x2b, x2, B22, ln["C"].norm, ln["D"].y, sig.x2b_ready)
                    if f:
                        residual3(it)
                    if c:
                        rsqrt_var(it, "C", "C")
                    if f:
                        rsqrt_var(it, "F", "F")
                    if c:
                        split(it, "C", x2, x2_hi, x2_lo, sig.agg2_done, ln["C"].norm, sig.x2_hi_done, sig.x2_split)
                    if d:
                        rsqrt_var(it, "D", "D")

                identity()
                run_iterations(pool, B, body, [("B", 0)])


_INS = ["x", "adj", "L0_gnn_fc_w", "L0_gnn_fc_b", "L0_gnn_q_w", "L0_gnn_q_b", "L0_gnn_k_w", "L0_gnn_k_b",
        "L0_gnn_fp_w", "L0_gnn_fp_b", "L1_gnn_eps", "L1_gnn_W1", "L1_gnn_b1", "L1_gnn_W2", "L1_gnn_b2",
        "L2_gnn_epsilon", "L2_gnn_W1", "L2_gnn_b1", "L2_gnn_rms_weight", "L2_gnn_W2", "L2_gnn_b2",
        "L3_gnn_W", "L3_gnn_a"]


def kernel(**inputs):
    import numpy as _np
    import concourse.bacc as _bacc
    from concourse import mybir as _mybir
    from concourse.bass_utils import run_bass_kernel_spmd as _run

    nc = _bacc.Bacc("TRN2", target_bir_lowering=False, num_devices=1)
    arrays, args = {}, []
    laid_out = {
        "L0_gnn_fc_b": lambda v: v.reshape(H0, P).T,
        "L1_gnn_b1": lambda v: v.reshape(HID1 // P, P).T,
        "L3_gnn_a": lambda v: v.reshape(H3, 2, D3).transpose(0, 2, 1).reshape(P, 2),
    }
    for name in _INS:
        a = _np.asarray(inputs[name])
        a = _np.ascontiguousarray(laid_out[name](a) if name in laid_out else a)
        a = a.reshape(a.shape or (1,))
        arrays[f"in_{name}_dram"] = a
        args.append(nc.dram_tensor(f"in_{name}_dram", a.shape, _mybir.dt.from_np(a.dtype), kind="ExternalInput").ap())
    out = nc.dram_tensor("out_dram", inputs["x"].shape, _mybir.dt.float32, kind="ExternalOutput").ap()
    gnn_stack(nc, *args, out)
    r = _run(nc, [arrays], core_ids=[0])
    return r.results[0]["out_dram"]
```
